# Optimizing a Trainium2 kernel written in Bass

```python
import numpy as np
import jax
import jax.numpy as jnp

def _softmax(x, axis=-1):
    return jax.nn.softmax(x, axis=axis)

def _gelu(x):
    return jax.nn.gelu(x, approximate=True)

def _silu(x):
    return jax.nn.silu(x)

def _sigmoid(x):
    return jax.nn.sigmoid(x)

def _layernorm(x, axis=-1, eps=1e-05):
    m = jnp.mean(x, axis=axis, keepdims=True)
    v = jnp.var(x, axis=axis, keepdims=True)
    return (x - m) / jnp.sqrt(v + eps)

def _scatter_add(tgt, idx, src, axis=0):
    return tgt.at[idx].add(src)

def _segment_sum(src, seg, n):
    return jax.ops.segment_sum(src, seg, n)
kernel_name = 'mk_seq_postln_d1_jaxref_r4_4c2e28'

def setup_inputs(seed: int=0):
    np.random.seed(seed)
    _w = jnp.asarray

    def _L0_attn_setup():
        import jax, jax.numpy as jnp
        import numpy as np
        import math
        BLK = 32
        D_MODEL = 256
        N_HEADS = 16
        HEAD_DIM = D_MODEL // N_HEADS
        SEQ_LEN = 1024
        BATCH = 2
        NUM_BLOCK = SEQ_LEN // BLK * 8
        DIAG_PRIOR = 3
        SCALE = 1.0 / math.sqrt(HEAD_DIM)

        def _mra2_full(Q, K, V):
            Bm, L, hd = Q.shape
            n = L // BLK
            Qb = Q.reshape(Bm, n, BLK, hd)
            Kb = K.reshape(Bm, n, BLK, hd)
            Vb = V.reshape(Bm, n, BLK, hd)
            Qh, Kh, Vh = (Qb.mean(2), Kb.mean(2), Vb.mean(2))
            low = jnp.einsum('bnd,bmd->bnm', Qh, Kh) * SCALE
            row_max = low.max(-1, keepdims=True)
            norm = jax.lax.stop_gradient(low - row_max)
            off = DIAG_PRIOR // 2
            ii = jnp.arange(n)
            band = (jnp.abs(ii[:, None] - ii[None, :]) <= off).astype(norm.dtype)
            norm = norm + band[None] * 5000.0
            top_vals, idx = jax.lax.top_k(norm.reshape(Bm, n * n), NUM_BLOCK)
            thresh = top_vals[:, -1]
            hi_mask = (norm >= thresh[:, None, None]).astype(norm.dtype)
            qblk = idx // n
            kblk = idx % n
            bidx = jnp.arange(Bm)[:, None]
            Qs = Qb[bidx, qblk]
            Ks = Kb[bidx, kblk]
            Vs = Vb[bidx, kblk]
            hi = jnp.einsum('bnqd,bnkd->bnqk', Qs, Ks) * SCALE
            blk_rmax = jax.lax.stop_gradient(hi.max(-1))
            max_vals = jnp.full((Bm, n, BLK), -1000000000.0, hi.dtype).at[bidx, qblk].max(blk_rmax)
            attn = jnp.exp(hi - max_vals[bidx, qblk][..., None])
            hi_out = jnp.zeros((Bm, n, BLK, hd), hi.dtype).at[bidx, qblk].add(jnp.einsum('bnqk,bnkd->bnqd', attn, Vs)).reshape(Bm, L, hd)
            hi_norm = jnp.zeros((Bm, n, BLK), hi.dtype).at[bidx, qblk].add(attn.sum(-1)).reshape(Bm, L)
            low_attn = jnp.exp(low - row_max - 10000.0 * hi_mask) * BLK
            low_out = jnp.einsum('bnm,bmd->bnd', low_attn, Vh)
            low_out = jnp.broadcast_to(low_out[:, :, None, :], (Bm, n, BLK, hd)).reshape(Bm, L, hd)
            low_norm = jnp.broadcast_to(low_attn.sum(-1)[:, :, None], (Bm, n, BLK)).reshape(Bm, L)
            rm = jnp.broadcast_to(row_max, (Bm, n, BLK)).reshape(Bm, L)
            log_corr = rm - max_vals.reshape(Bm, L)
            low_corr = jnp.exp(jnp.minimum(log_corr, 0.0))
            hi_corr = jnp.exp(-jnp.maximum(log_corr, 0.0))
            num = hi_out * hi_corr[..., None] + low_out * low_corr[..., None]
            den = hi_norm * hi_corr + low_norm * low_corr + 1e-06
            return num / den[..., None]
        key = jax.random.key(seed)
        kx, kq, kk, kv, kbq, kbk, kbv = jax.random.split(key, 7)
        bound = 1.0 / math.sqrt(D_MODEL)
        u = lambda k, shape: jax.random.uniform(k, shape, jnp.float32, -bound, bound)
        return {'X': jax.random.normal(kx, (BATCH, SEQ_LEN, D_MODEL), jnp.float32), 'Wq': u(kq, (D_MODEL, D_MODEL)), 'bq': u(kbq, (D_MODEL,)), 'Wk': u(kk, (D_MODEL, D_MODEL)), 'bk': u(kbk, (D_MODEL,)), 'Wv': u(kv, (D_MODEL, D_MODEL)), 'bv': u(kbv, (D_MODEL,))}
    _L0_attn_in = _L0_attn_setup()

    def _L0_ffn_setup():
        import jax, jax.numpy as jnp
        import numpy as np
        B, S, H, I, E, TOPK, KS = (4, 1024, 256, 128, 16, 2, 3)
        key = jax.random.key(seed)
        ks = jax.random.split(key, 9)
        sc = 0.02
        return {'hidden_states': jax.random.normal(ks[0], (B, S, H), dtype=jnp.float32), 'router_w': jax.random.normal(ks[1], (H, E), dtype=jnp.float32) * sc, 'router_bias': jnp.zeros((E,), dtype=jnp.float32), 'expert_gate_w': jax.random.normal(ks[2], (E - 1, H, I), dtype=jnp.float32) * sc, 'expert_up_w': jax.random.normal(ks[3], (E - 1, H, I), dtype=jnp.float32) * sc, 'expert_down_w': jax.random.normal(ks[4], (E - 1, I, H), dtype=jnp.float32) * sc, 'conv_w': jax.random.normal(ks[5], (I, H, KS), dtype=jnp.float32) * sc, 'shared_up_w': jax.random.normal(ks[6], (H, I), dtype=jnp.float32) * sc, 'shared_down_w': jax.random.normal(ks[7], (I, H), dtype=jnp.float32) * sc}
    _L0_ffn_in = _L0_ffn_setup()
    _d = {'L0_attn_X': _L0_attn_in['X'], 'L0_attn_Wq': _L0_attn_in['Wq'], 'L0_attn_bq': _L0_attn_in['bq'], 'L0_attn_Wk': _L0_attn_in['Wk'], 'L0_attn_bk': _L0_attn_in['bk'], 'L0_attn_Wv': _L0_attn_in['Wv'], 'L0_attn_bv': _L0_attn_in['bv'], 'L0_ffn_router_w': _L0_ffn_in['router_w'], 'L0_ffn_router_bias': _L0_ffn_in['router_bias'], 'L0_ffn_expert_gate_w': _L0_ffn_in['expert_gate_w'], 'L0_ffn_expert_up_w': _L0_ffn_in['expert_up_w'], 'L0_ffn_expert_down_w': _L0_ffn_in['expert_down_w'], 'L0_ffn_conv_w': _L0_ffn_in['conv_w'], 'L0_ffn_shared_up_w': _L0_ffn_in['shared_up_w'], 'L0_ffn_shared_down_w': _L0_ffn_in['shared_down_w']}
    _x0 = _d['L0_attn_X']
    _d['L0_attn_X'] = jax.random.normal(jax.random.fold_in(jax.random.key(seed), 1), (4, 2048, 256), dtype=_x0.dtype)
    del _x0
    return _d

def reference(L0_attn_X, L0_attn_Wq, L0_attn_bq, L0_attn_Wk, L0_attn_bk, L0_attn_Wv, L0_attn_bv, L0_ffn_router_w, L0_ffn_router_bias, L0_ffn_expert_gate_w, L0_ffn_expert_up_w, L0_ffn_expert_down_w, L0_ffn_conv_w, L0_ffn_shared_up_w, L0_ffn_shared_down_w):

    def _L0_attn_ref(X, Wq, bq, Wk, bk, Wv, bv):
        import jax, jax.numpy as jnp
        import numpy as np
        import math
        BLK = 32
        D_MODEL = 256
        N_HEADS = 16
        HEAD_DIM = D_MODEL // N_HEADS
        SEQ_LEN = 1024
        BATCH = 2
        NUM_BLOCK = SEQ_LEN // BLK * 8
        DIAG_PRIOR = 3
        SCALE = 1.0 / math.sqrt(HEAD_DIM)

        def _mra2_full(Q, K, V):
            Bm, L, hd = Q.shape
            n = L // BLK
            Qb = Q.reshape(Bm, n, BLK, hd)
            Kb = K.reshape(Bm, n, BLK, hd)
            Vb = V.reshape(Bm, n, BLK, hd)
            Qh, Kh, Vh = (Qb.mean(2), Kb.mean(2), Vb.mean(2))
            low = jnp.einsum('bnd,bmd->bnm', Qh, Kh) * SCALE
            row_max = low.max(-1, keepdims=True)
            norm = jax.lax.stop_gradient(low - row_max)
            off = DIAG_PRIOR // 2
            ii = jnp.arange(n)
            band = (jnp.abs(ii[:, None] - ii[None, :]) <= off).astype(norm.dtype)
            norm = norm + band[None] * 5000.0
            top_vals, idx = jax.lax.top_k(norm.reshape(Bm, n * n), NUM_BLOCK)
            thresh = top_vals[:, -1]
            hi_mask = (norm >= thresh[:, None, None]).astype(norm.dtype)
            qblk = idx // n
            kblk = idx % n
            bidx = jnp.arange(Bm)[:, None]
            Qs = Qb[bidx, qblk]
            Ks = Kb[bidx, kblk]
            Vs = Vb[bidx, kblk]
            hi = jnp.einsum('bnqd,bnkd->bnqk', Qs, Ks) * SCALE
            blk_rmax = jax.lax.stop_gradient(hi.max(-1))
            max_vals = jnp.full((Bm, n, BLK), -1000000000.0, hi.dtype).at[bidx, qblk].max(blk_rmax)
            attn = jnp.exp(hi - max_vals[bidx, qblk][..., None])
            hi_out = jnp.zeros((Bm, n, BLK, hd), hi.dtype).at[bidx, qblk].add(jnp.einsum('bnqk,bnkd->bnqd', attn, Vs)).reshape(Bm, L, hd)
            hi_norm = jnp.zeros((Bm, n, BLK), hi.dtype).at[bidx, qblk].add(attn.sum(-1)).reshape(Bm, L)
            low_attn = jnp.exp(low - row_max - 10000.0 * hi_mask) * BLK
            low_out = jnp.einsum('bnm,bmd->bnd', low_attn, Vh)
            low_out = jnp.broadcast_to(low_out[:, :, None, :], (Bm, n, BLK, hd)).reshape(Bm, L, hd)
            low_norm = jnp.broadcast_to(low_attn.sum(-1)[:, :, None], (Bm, n, BLK)).reshape(Bm, L)
            rm = jnp.broadcast_to(row_max, (Bm, n, BLK)).reshape(Bm, L)
            log_corr = rm - max_vals.reshape(Bm, L)
            low_corr = jnp.exp(jnp.minimum(log_corr, 0.0))
            hi_corr = jnp.exp(-jnp.maximum(log_corr, 0.0))
            num = hi_out * hi_corr[..., None] + low_out * low_corr[..., None]
            den = hi_norm * hi_corr + low_norm * low_corr + 1e-06
            return num / den[..., None]
        B, L, D = X.shape

        def heads(Y):
            return Y.reshape(B, L, N_HEADS, HEAD_DIM).transpose(0, 2, 1, 3).reshape(B * N_HEADS, L, HEAD_DIM)
        Q = heads(X @ Wq.T + bq)
        K = heads(X @ Wk.T + bk)
        V = heads(X @ Wv.T + bv)
        out = _mra2_full(Q, K, V)
        return out.reshape(B, N_HEADS, L, HEAD_DIM).transpose(0, 2, 1, 3).reshape(B, L, D)

    def _L0_ffn_ref(hidden_states, router_w, router_bias, expert_gate_w, expert_up_w, expert_down_w, conv_w, shared_up_w, shared_down_w):
        import jax, jax.numpy as jnp
        import numpy as np
        B, S, H, I, E, TOPK, KS = (4, 1024, 256, 128, 16, 2, 3)
        b, s, h = hidden_states.shape
        flat = hidden_states.reshape(b * s, h)
        logits = (flat @ router_w).astype(jnp.float32) + router_bias
        probs = jax.nn.softmax(logits, axis=-1)
        top_w, top_i = jax.lax.top_k(probs, TOPK)
        norm_w = top_w / (jnp.sum(top_w, axis=-1, keepdims=True) + 1e-06)
        norm_w = norm_w.astype(hidden_states.dtype)
        combine = jnp.sum(jax.nn.one_hot(top_i, E, dtype=norm_w.dtype) * norm_w[..., None], axis=1)
        routed = combine[:, E - 1:E] * flat
        for e in range(E - 1):
            y = jax.nn.silu(flat @ expert_gate_w[e]) * (flat @ expert_up_w[e]) @ expert_down_w[e]
            routed = routed + combine[:, e:e + 1] * y
        routed = routed.reshape(b, s, h)
        x_ncw = jnp.transpose(hidden_states, (0, 2, 1))
        gate = jax.lax.conv_general_dilated(x_ncw, conv_w, window_strides=(1,), padding=[(KS - 1, 0)], dimension_numbers=('NCW', 'OIW', 'NCW'))
        gate = jnp.transpose(gate, (0, 2, 1))
        shared = jax.nn.silu(gate) * (hidden_states @ shared_up_w) @ shared_down_w
        return shared + routed
    x = L0_attn_X
    x = _layernorm(x + _L0_attn_ref(x, L0_attn_Wq, L0_attn_bq, L0_attn_Wk, L0_attn_bk, L0_attn_Wv, L0_attn_bv), axis=-1)
    x = _layernorm(x + _L0_ffn_ref(x, L0_ffn_router_w, L0_ffn_router_bias, L0_ffn_expert_gate_w, L0_ffn_expert_up_w, L0_ffn_expert_down_w, L0_ffn_conv_w, L0_ffn_shared_up_w, L0_ffn_shared_down_w), axis=-1)
    return x

_drawn_inputs = setup_inputs


def setup_inputs(seed=0):
    import zlib

    import numpy as np

    out = dict(_drawn_inputs(seed))
    spreads = {'L0_ffn_router_bias': (0.0, 0.8)}
    factors = {'L0_attn_Wq': 8.0,
     'L0_attn_bq': 8.0,
     'L0_attn_Wk': 8.0,
     'L0_attn_bk': 64.0,
     'L0_attn_Wv': 4.12,
     'L0_ffn_router_w': 7.235,
     'L0_ffn_expert_gate_w': 7.201,
     'L0_ffn_expert_up_w': 7.109,
     'L0_ffn_expert_down_w': 7.11,
     'L0_ffn_conv_w': 2.819,
     'L0_ffn_shared_up_w': 2.717,
     'L0_ffn_shared_down_w': 2.732}
    for name, (base, spread) in spreads.items():
        noise = np.random.default_rng([zlib.crc32(name.encode()), seed]).standard_normal(out[name].shape)
        drawn = base * np.exp(spread * noise) if base else spread * noise
        out[name] = jnp.asarray(drawn.astype(out[name].dtype))
    for name, factor in factors.items():
        out[name] = (out[name] * factor).astype(out[name].dtype)
    return out
```

```python
from contextlib import ExitStack

import concourse.bass as bass
from concourse import mybir

ALU = mybir.AluOpType
ACT = mybir.ActivationFunctionType
F32 = mybir.dt.float32
BF16 = mybir.dt.bfloat16
AX_X = mybir.AxisListType.X
ds = bass.ds

P = 128
BATCH, SEQ, D = 4, 2048, 256
HEADS, HD = 16, 16
BLK = 32
NBLK = SEQ // BLK
PAIRS = 1024 // BLK * 8
NH = BATCH * HEADS
HALVES = D // P
CHUNK = 512
CPB = SEQ // CHUNK
NCHUNK = BATCH * CPB
SCALE = 0.25
BIG = 1e9
VW = 32
KT = SEQ // P
UNITS = (KT + 1) * CPB
GRP = NBLK // 2
EXPERTS, INNER, TAPS = 15, 128, 3
EPS_LN, EPS_DEN = 1e-5, 1e-6


def prepare(nc, t, scr):
    with ExitStack() as ctx:
        def sb(name, shape, dt=F32):
            return ctx.enter_context(nc.sbuf_tensor(name, shape, dt))

        def sem(name):
            return ctx.enter_context(nc.semaphore(name))

        XSLOTS = 4
        xt = sb("xt", [P, XSLOTS, HALVES, CHUNK])
        wq, wk, wv = (sb(n, [P, HALVES, D]) for n in ("wq", "wk", "wv"))
        bias_qk = sb("bias_qk", [P, 2, HALVES])
        bias_q = sb("bias_q", [P, HALVES])
        bias_head = sb("bias_head", [HD, 2, HEADS])
        bv_row = sb("bv_row", [1, D])
        ones_row = sb("ones_row", [1, P])
        blk_row = sb("blk_row", [1, NBLK])
        xsum = sb("xsum", [P, HALVES, BATCH * NBLK])
        qh = sb("qh", [HD, 2, HEADS, BATCH * NBLK])
        lows = sb("lows", [NBLK, NH * NBLK])
        x32 = sb("x32", [P, 2, CHUNK])
        parts = sb("parts", [P, 4, 3, CHUNK], BF16)
        vs = sb("vs", [P, 2, HEADS, 4, VW])
        vlow = sb("vlow", [NBLK, NH, VW])
        low = sb("low", [NH, NBLK * NBLK])
        norm = sb("norm", [NH, NBLK * NBLK])
        work = sb("work", [NH, NBLK * NBLK])
        maskb = sb("maskb", [NH, NBLK * NBLK], BF16)
        rm = sb("rm", [NH, NBLK])
        rm4 = sb("rm4", [NH, 4, KT])
        st = sb("st", [NH, 16])
        ge = lows

        ps_qk = ctx.enter_context(nc.psum_tensor("ps_qk", [P, 4, CHUNK], F32))
        ps_v = ctx.enter_context(nc.psum_tensor("ps_v", [P, 2, CHUNK], F32))
        ps_m = ctx.enter_context(nc.psum_tensor("ps_m", [P, 2, CHUNK], F32))

        w_in = sem("w_in")
        xt_in = [sem(f"xt_in{k}") for k in range(XSLOTS)]
        bias_ready = sem("bias_ready")
        rows_set, blocks_summed = sem("rows_set"), sem("blocks_summed")
        m_ready, m_free = sem("m_ready"), sem("m_free")
        qk_ready, x_ready = sem("qk_ready"), sem("x_ready")
        r1_done, p2_done, p3_done = sem("r1_done"), sem("p2_done"), sem("p3_done")
        parts_stored = [sem(f"parts_stored{u}") for u in range(4)]
        v_ready, v_packed, v_pad = sem("v_ready"), sem("v_packed"), sem("v_pad")
        v_stored = [sem(f"v_stored{u}") for u in range(2)]
        low_stored, low_in, sel = sem("low_stored"), sem("low_in"), sem("sel")
        masks_ready, out_stored = sem("masks_ready"), sem("out_stored")

        MU = 16
        LU = 8

        with nc.Block() as block:
            @block.sync
            def _(sp):
                for dst, src in ((wq, t["wq"]), (wk, t["wk"]), (wv, t["wv"]), (bias_qk, t["bias_qk"]),
                                 (bias_head, t["bias_head"]), (bv_row, t["bv"])):
                    sp.dma_start(dst[:], src).then_inc(w_in, 16)
                for k in range(NCHUNK):
                    if k >= XSLOTS:
                        sp.wait_ge(blocks_summed, k - XSLOTS + 1)
                    sp.dma_start(xt[:, k % XSLOTS], t["xt"][k]).then_inc(xt_in[k % XSLOTS], 16)
                sp.wait_ge(blocks_summed, NCHUNK)
                for k in range(XSLOTS):
                    sp.dma_start(xt[:, k], t["xt"][k]).then_inc(xt_in[k], 16)
                sp.wait_ge(m_free, 2 + MU + LU)
                sp.dma_start(scr["low"].rearrange("n q k -> q n k"),
                             lows[:].rearrange("q (n k) -> q n k", n=NH)).then_inc(low_stored, 16)
                sp.wait_ge(low_stored, 16)
                sp.dma_start(low[:], scr["low"].rearrange("n q k -> n (q k)")).then_inc(low_in, 16)

                def store_chunk(b, cc):
                    for u in range(4):
                        sp.wait_ge(p3_done, (b * CPB + cc) * 4 + u + 1 + 2)
                        dst = scr["q"] if u < 2 else scr["k"]
                        sp.dma_start(
                            dst[:, ds(b * D + (u % 2) * P, P), cc * CHUNK:(cc + 1) * CHUNK].rearrange("s p t -> p s t"),
                            parts[:, u]).then_inc(parts_stored[u], 16)
                    sp.wait_ge(v_packed, (b * CPB + cc + 1) * 2 + 2)
                    sp.dma_start(
                        scr["v"][ds(b * HEADS, HEADS), :, cc * 4:cc * 4 + 4].rearrange("h p t d -> p h (t d)"),
                        vs[:, cc % 2].rearrange("p h t d -> p h (t d)")).then_inc(v_stored[cc % 2], 16)

                with sp.Fori(0, BATCH - 1) as b:
                    for cc in range(CPB):
                        store_chunk(b, cc)
                        sp.wait_ge(v_ready, (b * CPB + cc + 1) * 2)
                        sp.dma_start(xt[:, cc], t["xt"][ds(b * CPB + cc + CPB, 1)].rearrange("o p a t -> (o p) a t"))\
                            .then_inc(xt_in[cc], 16)
                for cc in range(CPB):
                    store_chunk(BATCH - 1, cc)
                sp.wait_ge(m_free, 2 + MU + LU + BATCH)
                sp.dma_start(scr["vlow"].rearrange("n m d -> m n d"), vlow[:]).then_inc(out_stored, 16)
                sp.wait_ge(masks_ready, 1)
                sp.dma_start(scr["mask"].rearrange("n q k -> n (q k)"), maskb[:]).then_inc(out_stored, 16)
                sp.dma_start(scr["lowm"].rearrange("n q k -> n (q k)"), low[:]).then_inc(out_stored, 16)
                sp.dma_start(scr["rm"].rearrange("a n t -> n a t"), rm4[:]).then_inc(out_stored, 16)
                sp.wait_ge(out_stored, 16 * 4)
                for u in range(4):
                    sp.wait_ge(parts_stored[u], 16 * (NCHUNK + 1))
                for u in range(2):
                    sp.wait_ge(v_stored[u], 16 * (NCHUNK // 2 + 1))

            @block.gpsimd
            def _(pool):
                pool.sem_inc(p3_done, 2)
                nc.gpsimd.memset(ones_row[:], 1.0).then_inc(rows_set, 1)
                nc.gpsimd.memset(blk_row[:], float(BLK)).then_inc(rows_set, 1)
                nc.gpsimd.memset(vs[:], 0.0).then_inc(v_pad, 1)
                nc.gpsimd.memset(vlow[:], 0.0).then_inc(v_pad, 1)
                pool.wait_ge(v_pad, 2)
                nc.gpsimd.memset(vs[:, :, :, :, HD:HD + 1], 1.0).then_inc(v_pad, 1)
                nc.gpsimd.memset(vlow[:, :, HD:HD + 1], float(BLK)).then_inc(v_pad, 1)
                with pool.Fori(0, NCHUNK) as it:
                    for u in range(4):
                        n = it * 4 + u
                        xs = x32[:, u % 2]
                        pool.wait_ge(x_ready, n + 1 + 4)
                        nc.gpsimd.tensor_tensor(xs, xs, parts[:, u, 0], ALU.subtract).then_inc(r1_done, 1)
                        pool.wait_ge(p2_done, n + 1)
                        nc.gpsimd.tensor_tensor(parts[:, u, 2], xs, parts[:, u, 1], ALU.subtract).then_inc(p3_done, 1)

            @block.scalar
            def _(act):
                act.sem_inc(m_free, 2)
                act.sem_inc(x_ready, 4)
                act.sem_inc(v_packed, 2)
                for u in range(4):
                    act.sem_inc(parts_stored[u], 16)
                for u in range(2):
                    act.sem_inc(v_stored[u], 16)
                act.wait_ge(w_in, 16 * 6)
                nc.scalar.activation(bias_q[:], bias_qk[:, 0], ACT.Copy, scale=SCALE).then_inc(bias_ready, 1)
                act.wait_ge(bias_ready, 1)
                for u in range(MU):
                    act.wait_ge(m_ready, u + 1)
                    for i in range(2):
                        h = (u % 8) * 2 + i
                        last = nc.scalar.activation(qh[:, u // 8, h], ps_m[0:HD, u % 2, i * 256:(i + 1) * 256],
                                                    ACT.Identity, bias=bias_head[:, u // 8, h:h + 1], scale=1.0 / BLK)
                    last.then_inc(m_free, 1)
                for g in range(LU):
                    act.wait_ge(m_ready, MU + g + 1)
                    nc.scalar.activation(lows[:, g * 512:(g + 1) * 512], ps_m[0:NBLK, g % 2], ACT.Copy,
                                         scale=SCALE).then_inc(m_free, 1)
                act.wait_ge(v_pad, 4)
                for b in range(BATCH):
                    act.wait_ge(m_ready, MU + LU + b + 1)
                    nc.scalar.activation(vlow[:, b * HEADS:(b + 1) * HEADS, 0:HD],
                                         ps_m[0:NBLK, b % 2, 0:D].rearrange("p (h d) -> p h d", h=HEADS),
                                         ACT.Copy).then_inc(m_free, 1)

                def second_part(n, u):
                    act.wait_ge(r1_done, n + 1)
                    nc.scalar.activation(parts[:, u, 1], x32[:, u % 2], ACT.Copy).then_inc(p2_done, 1)

                with act.Fori(0, BATCH) as b:
                    for cc in range(CPB):
                        it = b * CPB + cc
                        for u in range(4):
                            n = it * 4 + u
                            act.wait_ge(qk_ready, n + 1)
                            act.wait_ge(parts_stored[u], (it + 1) * 16)
                            act.wait_ge(p3_done, n + 1)
                            bias, scale = (bias_q[:, u:u + 1], SCALE) if u < 2 else (bias_qk[:, 1, u - 2:u - 1], 1.0)
                            nc.scalar.activation(x32[:, u % 2], ps_qk[:, u], ACT.Identity, bias=bias, scale=scale)
                            nc.scalar.activation(parts[:, u, 0], ps_qk[:, u], ACT.Identity, bias=bias, scale=scale).then_inc(x_ready, 1)
                            if u:
                                second_part(n - 1, u - 1)
                        second_part(it * 4 + 3, 3)
                        act.wait_ge(v_stored[cc % 2], (b * 2 + cc // 2 + 1) * 16)
                        for j in range(2):
                            act.wait_ge(v_ready, it * 2 + j + 1)
                            nc.scalar.activation(
                                vs[:, cc % 2, :, 2 * j:2 * j + 2, 0:HD].rearrange("p h j d -> p j h d"),
                                ps_v[:, j].rearrange("p (j h d) -> p j h d", j=2, h=HEADS), ACT.Copy).then_inc(v_packed, 1)

            @block.vector
            def _(dve):
                for k in range(NCHUNK):
                    dve.wait_ge(xt_in[k % XSLOTS], 16 * (k // XSLOTS + 1))
                    nc.vector.reduce_sum(xsum[:, :, k * 16:(k + 1) * 16],
                                         xt[:, k % XSLOTS].rearrange("p a (n t) -> p a n t", t=BLK),
                                         AX_X).then_inc(blocks_summed, 1)
                steps = [0]

                def step(ins):
                    steps[0] += 1
                    ins.then_inc(sel, 1)
                    dve.wait_ge(sel, steps[0])

                T, U, SG, POS, V, CNT, C, K0, TH, NGE, NEQ, NEED, F, UJ, B2 = (st[:, i:i + 1] for i in range(15))
                dve.wait_ge(low_in, 16)
                low3 = low[:].rearrange("n (q k) -> n q k", q=NBLK)
                norm3 = norm[:].rearrange("n (q k) -> n q k", q=NBLK)
                step(nc.vector.reduce_max(rm[:], low3, AX_X))
                step(nc.vector.tensor_tensor(norm3, low3, rm[:].unsqueeze(2).to_broadcast([NH, NBLK, NBLK]), ALU.subtract))
                for s, n in ((0, NBLK), (1, NBLK - 1), (NBLK, NBLK - 1)):
                    d = norm[:, s:s + (NBLK + 1) * (n - 1) + 1:NBLK + 1]
                    step(nc.vector.tensor_scalar(d, d, 5000.0, None, ALU.add))

                def count(v, out):
                    return nc.vector.tensor_scalar(maskb[:], norm[:], v, 0.0, ALU.is_ge, ALU.add, accum_out=out)

                def holds():
                    step(count(V, CNT))
                    step(nc.vector.tensor_scalar(C, CNT, PAIRS - 0.5, POS, ALU.is_ge, ALU.is_equal))

                step(nc.vector.memset(V, 0.0))
                step(count(V, CNT))
                step(nc.vector.tensor_scalar(POS, CNT, PAIRS - 0.5, None, ALU.is_ge))
                step(nc.vector.tensor_scalar(SG, POS, 2.0, -1.0, ALU.mult, ALU.add))
                step(nc.vector.memset(T, 2.0 ** -126))
                step(nc.vector.tensor_scalar(V, T, SG, None, ALU.mult))
                holds()
                step(nc.vector.tensor_copy(K0, C))
                for e in (127, 64, 32, 16, 8, 4, 2, 1):
                    step(nc.vector.tensor_scalar(V, T, 2.0 ** e, SG, ALU.mult, ALU.mult))
                    holds()
                    step(nc.vector.tensor_scalar(F, C, 2.0 ** e - 1.0, 1.0, ALU.mult, ALU.add))
                    step(nc.vector.tensor_tensor(T, T, F, ALU.mult))
                step(nc.vector.tensor_copy(U, T))
                step(nc.vector.tensor_copy(UJ, T))
                base, per_bit = steps[0], 5
                with dve.Fori(0, 23) as j:
                    done = [0]

                    def turn(ins):
                        done[0] += 1
                        ins.then_inc(sel, 1)
                        dve.wait_ge(sel, base + j * per_bit + done[0])

                    turn(nc.vector.tensor_scalar(UJ, UJ, 0.5, None, ALU.mult))
                    turn(nc.vector.tensor_scalar(V, UJ, T, SG, ALU.add, ALU.mult))
                    turn(count(V, CNT))
                    turn(nc.vector.tensor_scalar(C, CNT, PAIRS - 0.5, POS, ALU.is_ge, ALU.is_equal))
                    turn(nc.vector.scalar_tensor_tensor(T, C, UJ, T, ALU.mult, ALU.add))
                steps[0] = base + 23 * per_bit
                step(nc.vector.tensor_scalar(F, U, 2.0 ** -23, K0, ALU.mult, ALU.mult))
                step(nc.vector.tensor_scalar(B2, F, T, -1.0, ALU.add, ALU.mult))
                step(nc.vector.tensor_tensor(V, T, K0, ALU.mult))
                step(nc.vector.tensor_tensor(V, V, POS, ALU.mult))
                step(nc.vector.tensor_scalar(F, POS, -1.0, 1.0, ALU.mult, ALU.add))
                step(nc.vector.tensor_tensor(B2, B2, F, ALU.mult))
                step(nc.vector.tensor_tensor(TH, V, B2, ALU.add))
                step(nc.vector.tensor_scalar(ge[:], norm[:], TH, 0.0, ALU.is_ge, ALU.add, accum_out=NGE))
                step(nc.vector.scalar_tensor_tensor(low[:], ge[:], -BIG, low[:], ALU.mult, ALU.add))
                step(nc.vector.tensor_scalar(norm[:], norm[:], TH, 0.0, ALU.is_equal, ALU.add, accum_out=NEQ))
                step(nc.vector.tensor_tensor(NEED, NEQ, NGE, ALU.subtract))
                step(nc.vector.tensor_scalar(NEED, NEED, float(PAIRS), None, ALU.add))
                step(nc.vector.tensor_tensor_scan(work[:], norm[:], norm[:], 0.0, ALU.add, ALU.max))
                step(nc.vector.scalar_tensor_tensor(work[:], work[:], NEED, norm[:], ALU.is_le, ALU.mult))
                step(nc.vector.tensor_tensor(work[:], work[:], norm[:], ALU.subtract))
                step(nc.vector.tensor_tensor(work[:], work[:], ge[:], ALU.add))
                step(nc.vector.tensor_copy(rm4[:], rm[:].rearrange("n (t a) -> n a t", a=4)))
                nc.vector.tensor_scalar(maskb[:], work[:], -1.0, BIG, ALU.add, ALU.mult).then_inc(masks_ready, 1)

            @block.tensor
            def _(pe):
                pe.wait_ge(w_in, 16 * 6)
                pe.wait_ge(rows_set, 2)
                pe.wait_ge(blocks_summed, NCHUNK)
                for u in range(MU):
                    pe.wait_ge(m_free, u + 1)
                    w = (wq, wk)[u // 8]
                    for i in range(2):
                        h = (u % 8) * 2 + i
                        for a in range(HALVES):
                            last = nc.tensor.matmul(ps_m[0:HD, u % 2, i * 256:(i + 1) * 256], w[:, a, h * HD:(h + 1) * HD],
                                                    xsum[:, a], start=(a == 0), stop=(a == HALVES - 1))
                    last.then_inc(m_ready, 1)
                pe.wait_ge(m_free, 2 + MU)
                for g in range(LU):
                    pe.wait_ge(m_free, MU + g + 1)
                    for i in range(8):
                        b, h = divmod(g * 8 + i, HEADS)
                        last = nc.tensor.matmul(ps_m[0:NBLK, g % 2, i * NBLK:(i + 1) * NBLK],
                                                qh[:, 0, h, b * NBLK:(b + 1) * NBLK], qh[:, 1, h, b * NBLK:(b + 1) * NBLK],
                                                start=True, stop=True)
                    last.then_inc(m_ready, 1)
                for b in range(BATCH):
                    pe.wait_ge(m_free, MU + LU + b + 1)
                    out = ps_m[0:NBLK, b % 2, 0:D]
                    for a in range(HALVES):
                        nc.tensor.matmul(out, xsum[:, a, b * NBLK:(b + 1) * NBLK], wv[:, a], start=(a == 0), stop=False)
                    nc.tensor.matmul(out, blk_row[:], bv_row[:], start=False, stop=True).then_inc(m_ready, 1)
                with pe.Fori(0, BATCH) as b:
                    for cc in range(CPB):
                        it = b * CPB + cc
                        pe.wait_ge(xt_in[cc], (b + 1 + NCHUNK // XSLOTS) * 16)
                        for u in range(4):
                            pe.wait_ge(x_ready, it * 4 + u + 1)
                            w = (wq, wk)[u // 2]
                            for a in range(HALVES):
                                last = nc.tensor.matmul(ps_qk[:, u], w[:, a, (u % 2) * P:(u % 2 + 1) * P], xt[:, cc, a],
                                                        start=(a == 0), stop=(a == HALVES - 1))
                            last.then_inc(qk_ready, 1)
                        for j in range(2):
                            pe.wait_ge(v_packed, it * 2 + j + 1)
                            for i in range(2):
                                out = ps_v[:, j, i * D:(i + 1) * D]
                                tok = slice((2 * j + i) * P, (2 * j + i + 1) * P)
                                for a in range(HALVES):
                                    nc.tensor.matmul(out, xt[:, cc, a, tok], wv[:, a], start=(a == 0), stop=False)
                                last = nc.tensor.matmul(out, ones_row[:], bv_row[:], start=False, stop=True)
                            last.then_inc(v_ready, 1)


def attend(nc, t, scr, att):
    with ExitStack() as ctx:
        def sb(name, shape, dt=F32):
            return ctx.enter_context(nc.sbuf_tensor(name, shape, dt))

        def sem(name):
            return ctx.enter_context(nc.semaphore(name))

        SLOTS = 3
        HALFK = SEQ // 2
        MASK = slice(2 * GRP, 3 * GRP)
        qa, qb, ka = (sb(n, [P, SLOTS, SEQ], BF16) for n in ("qa", "qb", "ka"))
        v = sb("v", [P, SLOTS, KT + 1, VW])
        lw = sb("lw", [3 * GRP, SLOTS, NBLK])
        mask_in = sb("mask_in", [NBLK, NH, NBLK], BF16)
        mta, mtb = (sb(n, [3 * GRP, NH + 1, NBLK], BF16) for n in ("mta", "mtb"))
        spread = sb("spread", [3 * GRP, SEQ])
        onehot = sb("onehot", [GRP, SEQ], BF16)
        ident = sb("ident", [P, P], BF16)
        identf = sb("identf", [GRP, GRP])
        fold = sb("fold", [P, VW])
        rmx = sb("rmx", [P, NH * KT])
        mx = sb("mx", [P, SLOTS, 2, KT])
        mfull = sb("mfull", [P, SLOTS, KT])
        mb = sb("mb", [P, SLOTS, KT], BF16)
        md = sb("md", [P, SLOTS, KT])
        me = sb("me", [P, SLOTS, KT])
        pt = sb("pt", [P, 4, CHUNK])
        os_ = sb("os_", [P, 2, CHUNK])
        den = sb("den", [P, 2, CPB])

        s1 = ctx.enter_context(nc.psum_tensor("s1", [P, 2, HALFK], F32))
        s2 = ctx.enter_context(nc.psum_tensor("s2", [P, 2, CHUNK], F32))
        acc = ctx.enter_context(nc.psum_tensor("acc", [P, 2, CHUNK], F32))

        start_in, consts, const2 = sem("start_in"), sem("consts"), sem("const2")
        mt_ready, mt_done = sem("mt_ready"), sem("mt_done")
        head_in = [sem(f"head_in{k}") for k in range(SLOTS)]
        expanded = sem("expanded")
        shifted = sem("shifted")
        s1_ready, s1_free = sem("s1_ready"), sem("s1_free")
        half_max, full_max, rounded, mb_ready = sem("half_max"), sem("full_max"), sem("rounded"), sem("mb_ready")
        s2_ready, s2_free = sem("s2_ready"), sem("s2_free")
        pv_done = sem("pv_done")
        os_ready, o_ready, den_done, rec_done, acc_free = (sem(n) for n in ("os_ready", "o_ready", "den_done", "rec_done", "acc_free"))
        pool_step = sem("pool_step")

        ROWS = 18
        HEAD_IN = 16 * (ROWS + 3)
        BPOS = (18, 33, 48, 63)
        RING = UNITS + CPB
        TILES = 2 * KT

        def pos(r):
            return r + sum(x < r for x in BPOS)

        def pass1_units(r):
            return [u for u in range(TILES) if u * 60 // TILES == r]

        with nc.Block() as block:
            @block.sync
            def _(sp):
                for a in range(4):
                    src = scr["rm"][a].rearrange("n t -> (n t)").unsqueeze(0).to_broadcast([GRP, NH * KT])
                    sp.dma_start(rmx[a * GRP:(a + 1) * GRP], src).then_inc(start_in, 16)
                sp.dma_start(mask_in[:], scr["mask"].rearrange("n q k -> q n k")).then_inc(start_in, 16)

                def load(m, slot):
                    def rows(dst, at, src, part):
                        sp.dma_start(dst[at:at + HD, slot], src[part, ds(m * HD, HD)]).then_inc(head_in[slot], 16)

                    for at, pq, pk in ((0, 0, 0), (16, 0, 1), (32, 1, 0), (48, 1, 1), (96, 0, 2), (112, 2, 0)):
                        rows(qa, at, scr["q"], pq)
                        rows(qb, at, scr["q"], pq)
                        rows(ka, at, scr["k"], pk)
                    one = ds(m, 1)
                    sp.dma_start(v[:, slot, 0:KT], scr["v"][one].rearrange("o p t d -> (o p) t d")).then_inc(head_in[slot], 16)
                    sp.dma_start(v[0:NBLK, slot, KT], scr["vlow"][one].rearrange("o m d -> (o m) d")).then_inc(head_in[slot], 16)
                    sp.dma_start(lw[0:NBLK, slot], scr["lowm"][one].rearrange("o q k -> (o q) k")).then_inc(head_in[slot], 16)

                load(0, 0)
                load(1, 1)
                with sp.Fori(0, (NH - 1) // SLOTS - 1) as i:
                    for j in range(SLOTS):
                        n = i * SLOTS + j
                        sp.wait_ge(pv_done, n * UNITS + 4)
                        load(n + 2, (j + 2) % SLOTS)
                for n in range(NH - 4, NH - 2):
                    sp.wait_ge(pv_done, n * UNITS + 4)
                    load(n + 2, (n + 2) % SLOTS)

            @block.gpsimd
            def _(pool):
                nc.gpsimd.memset(ident[:], 0.0).then_inc(consts, 1)
                nc.gpsimd.memset(identf[:], 0.0).then_inc(consts, 1)
                nc.gpsimd.memset(spread[:], 0.0).then_inc(consts, 1)
                nc.gpsimd.memset(onehot[:], 0.0).then_inc(consts, 1)
                pool.wait_ge(consts, 4 + 3)

                def diagonal(ap, pattern):
                    return nc.gpsimd.affine_select(out=ap, in_=ap, compare_op=ALU.not_equal, fill=1.0, base=0,
                                                   pattern=pattern, channel_multiplier=1)

                diagonal(ident[:], [[-1, P]]).then_inc(const2, 1)
                diagonal(identf[:], [[-1, GRP]]).then_inc(const2, 1)
                diagonal(spread[0:NBLK].rearrange("p (b t) -> p b t", t=BLK), [[-1, NBLK], [0, BLK]]).then_inc(const2, 1)
                diagonal(onehot[:].rearrange("p (g b t) -> p g b t", g=2, t=BLK), [[0, 2], [-1, GRP], [0, BLK]]).then_inc(const2, 1)

                def expand(m, slot):
                    for q, mt in ((qa, mta), (qb, mtb)):
                        one = mt[MASK, ds(m, 1)].rearrange("p o b -> p (o b)")
                        last = nc.gpsimd.tensor_copy(q[MASK, slot].rearrange("p (b t) -> p b t", t=BLK),
                                                     one.unsqueeze(2).to_broadcast([GRP, NBLK, BLK]))
                    last.then_inc(expanded, 1)

                def shift(m, slot, c, ring):
                    pool.wait_ge(s2_free, ring + 1 + 2)
                    for q in (qa, qb):
                        part = q[MASK, slot, c * CHUNK:(c + 1) * CHUNK]
                        last = nc.gpsimd.tensor_tensor(part, part, spread[MASK, c * CHUNK:(c + 1) * CHUNK], ALU.subtract)
                    last.then_inc(shifted, 1)

                pool.wait_ge(mt_done, 16)
                expand(0, 0)
                expand(1, 1)
                for c in range(CPB):
                    shift(0, 0, c, c)
                with pool.Fori(0, (NH - 1) // SLOTS) as i:
                    for j in range(SLOTS):
                        n = i * SLOTS + j
                        pool.wait_ge(pv_done, n * UNITS + 4)
                        expand(n + 2, (j + 2) % SLOTS)
                        for c in range(CPB):
                            shift(n + 1, (j + 1) % SLOTS, c, CPB + n * RING + BPOS[c] + 1 + c)

            @block.scalar
            def _(act):
                act.sem_inc(s2_free, 2)

                def shift(m, slot, c, ring, bank):
                    act.wait_ge(mb_ready, m * CPB + c + 1)
                    cols = slice(c * 4, c * 4 + 4)
                    nc.scalar.activation(me[:, slot, cols], md[:, slot, cols], ACT.Exp)
                    act.wait_ge(s2_ready, ring + 1)
                    nc.scalar.activation(spread[MASK, c * CHUNK:(c + 1) * CHUNK], s2[MASK, bank],
                                         ACT.Copy).then_inc(s2_free, 1)

                def step(n, j, nxt):
                    for r in range(UNITS):
                        p = pos(r) if nxt else r
                        act.wait_ge(s2_ready, CPB + n * RING + p + 1)
                        act.wait_ge(pv_done, n * UNITS + r + 1)
                        rows = slice(0, NBLK) if r % (KT + 1) == 0 else slice(0, P)
                        nc.scalar.activation(pt[rows, r % 4], s2[rows, p % 2], ACT.Exp).then_inc(s2_free, 1)
                        if nxt and r in BPOS:
                            c = BPOS.index(r)
                            shift(n + 1, (j + 1) % SLOTS, c, CPB + n * RING + p + 1, (p + 1) % 2)

                act.wait_ge(const2, 7)
                for c in range(CPB):
                    shift(0, 0, c, c, c % 2)
                with act.Fori(0, (NH - 1) // SLOTS) as i:
                    for j in range(SLOTS):
                        step(i * SLOTS + j, j, True)
                step(NH - 1, 0, False)

            @block.vector
            def _(dve):
                dve.sem_inc(s1_free, 2)
                dve.sem_inc(acc_free, 2)
                nc.vector.memset(mta[MASK, NH], 0.0).then_inc(consts, 1)
                nc.vector.memset(mtb[MASK, NH], 0.0).then_inc(consts, 1)
                nc.vector.memset(lw[MASK], 0.0).then_inc(consts, 1)
                nc.vector.memset(v[NBLK:P, :, KT], 0.0).then_inc(const2, 1)
                nc.vector.memset(pt[:], 0.0).then_inc(const2, 1)
                dve.wait_ge(consts, 7)
                nc.vector.memset(lw[2 * GRP:2 * GRP + 1], -1.0).then_inc(const2, 1)
                for g in range(8):
                    dve.wait_ge(mt_ready, g + 1)
                    bank = s1[:].rearrange("p g (h c) -> p (g h) c", c=CHUNK)[:, g % 4]
                    for q, mt in enumerate((mta, mtb)):
                        nc.vector.tensor_copy(mt[MASK, g * 8:(g + 1) * 8].rearrange("p n b -> p (n b)"),
                                              bank[q * GRP:(q + 1) * GRP]).then_inc(mt_done, 1)
                dve.wait_ge(const2, 7)
                for k in range(SLOTS):
                    nc.vector.tensor_copy(ka[MASK, k], onehot[:])
                for a in range(4):
                    last = nc.vector.tensor_copy(fold[a * GRP:(a + 1) * GRP], identf[:])
                last.then_inc(consts, 1)
                dve.wait_ge(start_in, 16 * 5)

                def row_max(m, slot, u):
                    dve.wait_ge(s1_ready, m * TILES + u + 1)
                    nc.vector.reduce_max(mx[:, slot, u % 2, u // 2:u // 2 + 1], s1[:, u % 2], AX_X).then_inc(s1_free, 1)

                def maxima(m, slot, c):
                    k, cols = m * CPB + c + 1, slice(c * 4, c * 4 + 4)
                    dve.wait_ge(s1_free, m * TILES + 8 * c + 8 + 2)
                    nc.vector.tensor_tensor(mfull[:, slot, cols], mx[:, slot, 0, cols], mx[:, slot, 1, cols], ALU.max).then_inc(half_max, 1)
                    dve.wait_ge(half_max, k)
                    nc.vector.tensor_tensor(mfull[:, slot, cols], mfull[:, slot, cols], rmx[:, ds(m * KT + c * 4, 4)], ALU.max).then_inc(full_max, 1)
                    dve.wait_ge(full_max, k)
                    nc.vector.tensor_copy(mb[:, slot, cols], mfull[:, slot, cols]).then_inc(rounded, 1)
                    dve.wait_ge(rounded, k)
                    nc.vector.tensor_tensor(md[:, slot, cols], mfull[:, slot, cols], mb[:, slot, cols], ALU.subtract).then_inc(mb_ready, 1)

                def evacuate(n, c):
                    dve.wait_ge(pv_done, 4 + n * UNITS + (c + 1) * (KT + 1))
                    nc.vector.tensor_copy(os_[:, c % 2], acc[:, c % 2]).then_inc(os_ready, 1)

                def normalise(n, slot, c):
                    k, cols = n * CPB + c + 1, slice(c * 4, c * 4 + 4)
                    dve.wait_ge(o_ready, k)
                    o = acc[:, c % 2, 0:4 * VW].rearrange("p (j d) -> p j d", d=VW)
                    nc.vector.scalar_tensor_tensor(den[:, 0], me[:, slot, cols], EPS_DEN,
                                                   o[:, :, HD:HD + 1].rearrange("p j d -> p (j d)"), ALU.mult, ALU.add).then_inc(den_done, 1)
                    dve.wait_ge(den_done, k)
                    nc.vector.reciprocal(den[:, 1], den[:, 0]).then_inc(rec_done, 1)
                    dve.wait_ge(rec_done, k)
                    dst = att[:, ds(n, 1), cols].rearrange("p o j d -> p (o j) d")
                    nc.vector.tensor_tensor(dst, o[:, :, 0:HD], den[:, 1].unsqueeze(2).to_broadcast([P, 4, HD]), ALU.mult).then_inc(acc_free, 1)

                def step(n, j, nxt, before, flush):
                    for r in range(UNITS):
                        c, k = divmod(r, KT + 1)
                        if nxt:
                            for u in pass1_units(r):
                                row_max(n + 1, (j + 1) % SLOTS, u)
                                if u % 8 == 7:
                                    maxima(n + 1, (j + 1) % SLOTS, u // 8)
                        if k == 3 and c:
                            evacuate(n, c - 1)
                        elif k == 3 and before:
                            evacuate(n - 1, CPB - 1)
                        if k == 8 and c:
                            normalise(n, j, c - 1)
                        elif k == 8 and before:
                            normalise(n - 1, (j - 1) % SLOTS, CPB - 1)
                    if flush:
                        evacuate(n, CPB - 1)
                        normalise(n, j, CPB - 1)

                for u in range(TILES):
                    row_max(0, 0, u)
                    if u % 8 == 7:
                        maxima(0, 0, u // 8)
                with dve.Fori(0, (NH - 1) // SLOTS) as i:
                    for j in range(SLOTS):
                        step(i * SLOTS + j, j, True, j > 0, j == SLOTS - 1)
                step(NH - 1, 0, False, False, True)

            @block.tensor
            def _(pe):
                pe.sem_inc(pv_done, 4)
                pe.wait_ge(const2, 7)
                pe.wait_ge(start_in, 16 * 5)
                for g in range(8):
                    if g >= 4:
                        pe.wait_ge(mt_done, 2 * (g - 3))
                    bank = s1[:].rearrange("p g (h c) -> p (g h) c", c=CHUNK)[:, g % 4]
                    for i in range(8):
                        last = nc.tensor.matmul(bank[0:NBLK, i * NBLK:(i + 1) * NBLK], mask_in[:, g * 8 + i],
                                                ident[0:NBLK, 0:NBLK], start=True, stop=True)
                    last.then_inc(mt_ready, 1)
                pe.wait_ge(mt_done, 16)
                pe.wait_ge(consts, 8)

                def tile1(m, slot, u):
                    tq, g = divmod(u, 2)
                    pe.wait_ge(s1_free, m * TILES + u + 1)
                    for i in range(HALFK // CHUNK):
                        k0 = g * HALFK + i * CHUNK
                        last = nc.tensor.matmul(s1[:, g, i * CHUNK:(i + 1) * CHUNK], (qa, qb)[g][:, slot, tq * P:(tq + 1) * P],
                                                ka[:, slot, k0:k0 + CHUNK], start=True, stop=True)
                    last.then_inc(s1_ready, 1)

                def tile2(n, slot, r, p):
                    c, k = divmod(r, KT + 1)
                    cols = slice(c * CHUNK, (c + 1) * CHUNK)
                    if k == 0:
                        pe.wait_ge(shifted, n * CPB + c + 1)
                    pe.wait_ge(s2_free, CPB + n * RING + p + 1)
                    if k == 0:
                        mm = nc.tensor.matmul(s2[0:NBLK, p % 2], lw[:, slot], spread[:, cols], start=True, stop=True)
                    else:
                        q = qa if k <= KT // 2 else qb
                        mm = nc.tensor.matmul(s2[:, p % 2], ka[:, slot, (k - 1) * P:k * P], q[:, slot, cols], start=True, stop=True)
                    mm.then_inc(s2_ready, 1)

                def shift(m, slot, c, ring, bank):
                    pe.wait_ge(mb_ready, m * CPB + c + 1)
                    pe.wait_ge(s2_free, ring + 1)
                    for i in range(4):
                        tq = c * 4 + i
                        last = nc.tensor.matmul(s2[MASK, bank, i * P:(i + 1) * P], mb[:, slot, tq:tq + 1].to_broadcast([P, GRP]),
                                                ident[:], start=True, stop=True)
                    last.then_inc(s2_ready, 1)

                def times_v(n, slot, r, p):
                    c, k = divmod(r, KT + 1)
                    pe.wait_ge(s2_free, CPB + n * RING + p + 1 + 2)
                    if k == 0:
                        pe.wait_ge(acc_free, n * CPB + c + 1)
                    g = k % 4
                    mm = nc.tensor.matmul(acc[g * VW:(g + 1) * VW, c % 2], v[:, slot, (k - 1) % (KT + 1)], pt[:, r % 4],
                                          start=(k < 4), stop=(k > KT - 4))
                    mm.then_inc(pv_done, 1)

                def fold_sums(n, c):
                    pe.wait_ge(os_ready, n * CPB + c + 1)
                    for i in range(4):
                        last = nc.tensor.matmul(acc[:, c % 2, i * VW:(i + 1) * VW], os_[:, c % 2, i * P:(i + 1) * P], fold[:],
                                                start=True, stop=True)
                    last.then_inc(o_ready, 1)

                def step(n, j, nxt, before, flush, turn=None):
                    if nxt:
                        pe.wait_ge(expanded, n + 2)
                        pe.wait_ge(head_in[(j + 1) % SLOTS], turn * HEAD_IN)
                    for r in range(UNITS):
                        c, k = divmod(r, KT + 1)
                        p = pos(r) if nxt else r
                        tile2(n, j, r, p)
                        if nxt:
                            for u in pass1_units(r):
                                tile1(n + 1, (j + 1) % SLOTS, u)
                            if r in BPOS:
                                shift(n + 1, (j + 1) % SLOTS, BPOS.index(r), CPB + n * RING + p + 1, (p + 1) % 2)
                        if r >= 2:
                            times_v(n, j, r - 2, pos(r - 2) if nxt else r - 2)
                        elif before:
                            times_v(n - 1, (j - 1) % SLOTS, UNITS - 2 + r, pos(UNITS - 2 + r))
                        if k == 6 and c:
                            fold_sums(n, c - 1)
                        elif k == 6 and before:
                            fold_sums(n - 1, CPB - 1)
                    if flush:
                        for r in (UNITS - 2, UNITS - 1):
                            times_v(n, j, r, pos(r) if nxt else r)
                        fold_sums(n, CPB - 1)

                pe.wait_ge(expanded, 1)
                pe.wait_ge(head_in[0], HEAD_IN)
                for u in range(TILES):
                    tile1(0, 0, u)
                for c in range(CPB):
                    shift(0, 0, c, c, c % 2)
                with pe.Fori(0, (NH - 1) // SLOTS) as i:
                    for j in range(SLOTS):
                        step(i * SLOTS + j, j, True, j > 0, j == SLOTS - 1, i + (j + 1) // SLOTS + 1)
                step(NH - 1, 0, False, False, True)


def ffn(nc, t, att, out):
    with ExitStack() as ctx:
        def sb(name, shape, dt=F32):
            return ctx.enter_context(nc.sbuf_tensor(name, shape, dt))

        def sem(name):
            return ctx.enter_context(nc.semaphore(name))

        TJ = CHUNK // P
        ITEMS = EXPERTS + 1
        RING = ITEMS + 2
        TURN_AFTER, ROUTE_AFTER = 8, 10
        gate_w = sb("gate_w", [P, EXPERTS, HALVES, INNER])
        up_w = sb("up_w", [P, EXPERTS, HALVES, INNER])
        down_w = sb("down_w", [INNER, EXPERTS, D])
        conv_w = sb("conv_w", [P, TAPS, HALVES, INNER])
        sup_w = sb("sup_w", [P, HALVES, INNER])
        sdown_w = sb("sdown_w", [INNER, D])
        router_w = sb("router_w", [P, HALVES, HEADS])
        router_b = sb("router_b", [1, HEADS])
        ones = sb("ones", [1, P])
        eps = sb("eps", [P, 1])
        zero = sb("zero", [P, HALVES, TAPS - 1])
        identity = sb("identity", [P, P])
        xin = sb("xin", [P, 2, TJ, D])
        x1 = sb("x1", [P, 2, TJ, D])
        xT = sb("xT", [P, 2, HALVES, TAPS - 1 + CHUNK])
        stats = sb("stats", [P, 2, TJ, 6])
        mv = sb("mv", [P, 2, TJ, 2])
        std = sb("std", [P, 2, TJ])
        rstd = sb("rstd", [P, 2, TJ])
        prob = sb("prob", [P, TJ, HEADS])
        comb = sb("comb", [P, 2, TJ, HEADS])
        gt, eq, rank = (sb(n, [P, TJ, HEADS]) for n in ("gt", "eq", "rank"))
        top = sb("top", [P, TJ, 8])
        col = sb("col", [P, 4, TJ])
        carrier = sb("carrier", [P, 1])
        sg = sb("sg", [P, 2, CHUNK])
        hh = sb("hh", [P, 2, CHUNK])
        ysum = sb("ysum", [P, TJ, D])
        y = sb("y", [P, 2, TJ, D])

        gu = ctx.enter_context(nc.psum_tensor("gu", [P, 2, 2, CHUNK], F32))
        yd = ctx.enter_context(nc.psum_tensor("yd", [P, 2, TJ, D], F32))

        w_in, consts = sem("ffn_w_in"), sem("ffn_consts")
        x_in = [sem(f"x_in{k}") for k in range(2)]
        y_out = [sem(f"y_out{k}") for k in range(2)]
        seq = sem("seq")
        gu_ready = sem("gu_ready")
        silu_done, h_ready, yd_ready, yd_free = (sem(n) for n in ("silu_done", "h_ready", "yd_ready", "yd_free"))
        var1, std1, var2, std2 = (sem(n) for n in ("var1", "std1", "var2", "std2"))
        x1_ready, xt_ready, logit_ready, exp_done = (sem(n) for n in ("x1_ready", "xt_ready", "logit_ready", "exp_done"))
        y_ready = sem("y_ready")

        def place(e):
            return e + (e > TURN_AFTER) + (e > ROUTE_AFTER)

        TURN, ROUTE = place(TURN_AFTER) + 1, place(ROUTE_AFTER) + 1
        FIRST = 2
        FRONT, TAIL = 16, 3
        PER = FRONT + TAIL

        with nc.Block() as block:
            @block.sync
            def _(sp):
                for dst, name in ((router_w, "router"), (router_b, "router_bias"), (gate_w, "gate"), (up_w, "up"),
                                  (down_w, "down"), (conv_w, "conv"), (sup_w, "shared_up"), (sdown_w, "shared_down")):
                    sp.dma_start(dst[:], t[name]).then_inc(w_in, 16)

                def tokens(ap, ch):
                    return ap[ds(ch * CHUNK, CHUNK)].rearrange("(j p) d -> p j d", p=P)

                def load(ch, s):
                    sp.dma_start(xin[:, s], tokens(t["x"], ch)).then_inc(x_in[s], 16)

                def store(ch, s):
                    sp.wait_ge(y_ready, ch + 1)
                    sp.dma_start(tokens(out, ch), y[:, s]).then_inc(y_out[s], 16)

                load(0, 0)
                load(1, 1)
                with sp.Fori(0, BATCH - 1) as b:
                    for cc in range(CPB):
                        store(b * CPB + cc, cc % 2)
                        load(b * CPB + cc + 2, cc % 2)
                for cc in range(CPB):
                    store(NCHUNK - CPB + cc, cc % 2)
                    if cc < 2:
                        load(NCHUNK - CPB + cc + 2, cc % 2)
                for s in range(2):
                    sp.wait_ge(y_out[s], 16 * (NCHUNK // 2 + 1))

            @block.gpsimd
            def _(pool):
                nc.gpsimd.memset(identity[:], 0.0).then_inc(consts, 1)
                nc.gpsimd.memset(ones[:], 1.0).then_inc(consts, 1)
                nc.gpsimd.memset(eps[:], EPS_LN).then_inc(consts, 1)
                nc.gpsimd.memset(zero[:], 0.0).then_inc(consts, 1)
                pool.wait_ge(consts, 4)
                nc.gpsimd.affine_select(out=identity[:], in_=identity[:], compare_op=ALU.not_equal, fill=1.0, base=0,
                                        pattern=[[-1, P]], channel_multiplier=1).then_inc(consts, 1)

            @block.scalar
            def _(act):
                for k in range(2):
                    act.sem_inc(y_out[k], 16)
                act.wait_ge(consts, 5)

                def root(var, ready, done, count, s):
                    act.wait_ge(ready, count)
                    nc.scalar.activation(std[:, s], var, ACT.Sqrt, bias=eps[:, 0:1]).then_inc(done, 1)

                def front_ln(ch, s):
                    root(mv[:, 0, :, 1], var1, std1, ch + 1, 0)

                def front_turn(ch, s, first, ring, slot):
                    act.wait_ge(gu_ready, ring + 1)
                    before = zero[:] if first else xT[:, 1 - s, :, CHUNK:CHUNK + TAPS - 1]
                    nc.scalar.activation(xT[:, s, :, 0:TAPS - 1], before, ACT.Copy)
                    nc.scalar.activation(xT[:, s, :, TAPS - 1:], gu[:, slot], ACT.Copy).then_inc(xt_ready, 1)

                def front_exp(ch):
                    act.wait_ge(logit_ready, ch + 1)
                    nc.scalar.activation(prob[:], prob[:], ACT.Exp).then_inc(exp_done, 1)

                def chunk(ch, s, nxt, first_next):
                    for e in range(ITEMS):
                        p = place(e) if nxt else e
                        act.wait_ge(gu_ready, FIRST + ch * RING + p + 1)
                        act.wait_ge(h_ready, ch * ITEMS + e + 1)
                        nc.scalar.activation(sg[:, e % 2], gu[:, p % 2, 0], ACT.Silu).then_inc(silu_done, 1)
                        if nxt and e == 4:
                            front_ln(ch + 1, 1 - s)
                        if nxt and e == TURN_AFTER:
                            front_turn(ch + 1, 1 - s, first_next, FIRST + ch * RING + TURN, TURN % 2)
                        if nxt and e == ROUTE_AFTER:
                            front_exp(ch + 1)
                    root(mv[:, 1, :, 1], var2, std2, ch + 1, 1)

                front_ln(0, 0)
                front_turn(0, 0, True, 0, 0)
                front_exp(0)
                with act.Fori(0, BATCH - 1) as b:
                    for cc in range(CPB):
                        chunk(b * CPB + cc, cc % 2, True, cc == CPB - 1)
                for cc in range(CPB):
                    chunk(NCHUNK - CPB + cc, cc % 2, cc < CPB - 1, False)

            @block.vector
            def _(dve):
                dve.sem_inc(h_ready, 2)
                dve.sem_inc(yd_free, 2)
                dve.wait_ge(w_in, 16 * 8)

                def normalise(dst, src, which, seq_at):
                    nc.vector.reciprocal(rstd[:, which], std[:, which]).then_inc(seq, 1)
                    dve.wait_ge(seq, seq_at)
                    for j in range(TJ):
                        last = nc.vector.tensor_scalar(dst[:, j], src[:, j], mv[:, which, j, 0:1], rstd[:, which, j:j + 1],
                                                       ALU.subtract, ALU.mult)
                    return last

                def variance(src, which, seq_at):
                    for j in range(TJ):
                        last = nc.vector.bn_stats(stats[:, which, j], src[:, j])
                    last.then_inc(seq, 1)
                    dve.wait_ge(seq, seq_at)
                    nc.vector.memset(carrier[:], 0.0)
                    for j in range(TJ):
                        last = nc.vector.bn_aggr(mv[:, which, j], stats[:, which, j])
                    return last

                def front_a(ch, b, cc, s, base):
                    dve.wait_ge(x_in[s], (b * 2 + cc // 2 + 1) * 16)
                    a = att[:, ds(b * HEADS, HEADS), cc * TJ:(cc + 1) * TJ].rearrange("p h j d -> p j h d")
                    nc.vector.tensor_tensor(x1[:, s].rearrange("p j (h d) -> p j h d", h=HEADS),
                                            xin[:, s].rearrange("p j (h d) -> p j h d", h=HEADS), a, ALU.add).then_inc(seq, 1)
                    dve.wait_ge(seq, base + 1)
                    variance(x1[:, s], 0, base + 2).then_inc(var1, 1)

                def front_b(ch, s, base):
                    dve.wait_ge(std1, ch + 1)
                    normalise(x1[:, s], x1[:, s], 0, base + 3).then_inc(x1_ready, 1)

                def front_c(ch, s, base, ring, slot):
                    dve.wait_ge(gu_ready, ring + 1)
                    lg = gu[:, slot, 0, 0:TJ * HEADS].rearrange("p (j e) -> p j e", j=TJ)
                    nc.vector.reduce_max(col[:, 0], lg, AX_X).then_inc(seq, 1)
                    dve.wait_ge(seq, base + 4)
                    nc.vector.tensor_tensor(prob[:], lg, col[:, 0].unsqueeze(2).to_broadcast([P, TJ, HEADS]),
                                            ALU.subtract).then_inc(logit_ready, 1)

                def front_d(ch, s, base):
                    done = [4]

                    def step(ins):
                        done[0] += 1
                        ins.then_inc(seq, 1)
                        dve.wait_ge(seq, base + done[0])

                    def wide(c):
                        return c.unsqueeze(2).to_broadcast([P, TJ, HEADS])

                    dve.wait_ge(exp_done, ch + 1)
                    step(nc.vector.reduce_sum(col[:, 0], prob[:], AX_X))
                    step(nc.vector.reciprocal(col[:, 1], col[:, 0]))
                    step(nc.vector.tensor_tensor(prob[:], prob[:], wide(col[:, 1]), ALU.mult))
                    nc.vector.memset(carrier[:], 0.0)
                    for j in range(TJ):
                        last = nc.vector.max(top[:, j], prob[:, j])
                    step(last)
                    second = top[:, :, 1]
                    nc.vector.tensor_tensor(gt[:], prob[:], wide(second), ALU.is_gt)
                    nc.vector.tensor_tensor(eq[:], prob[:], wide(second), ALU.is_equal)
                    step(nc.vector.tensor_tensor(col[:, 2], top[:, :, 0], second, ALU.add))
                    step(nc.vector.reduce_sum(col[:, 0], gt[:], AX_X))
                    for j in range(TJ):
                        nc.vector.tensor_tensor_scan(rank[:, j], eq[:, j], eq[:, j], 0.0, ALU.add, ALU.max)
                    nc.vector.tensor_scalar(col[:, 2], col[:, 2], 1e-6, None, ALU.add)
                    step(nc.vector.tensor_scalar(col[:, 0], col[:, 0], -1.0, 2.0, ALU.mult, ALU.add))
                    nc.vector.reciprocal(col[:, 3], col[:, 2])
                    step(nc.vector.tensor_tensor(rank[:], rank[:], wide(col[:, 0]), ALU.is_le))
                    step(nc.vector.tensor_tensor(rank[:], rank[:], eq[:], ALU.mult))
                    step(nc.vector.tensor_tensor(gt[:], gt[:], rank[:], ALU.add))
                    step(nc.vector.tensor_tensor(gt[:], gt[:], prob[:], ALU.mult))
                    step(nc.vector.tensor_tensor(comb[:, s], gt[:], wide(col[:, 3]), ALU.mult))
                    assert done[0] == FRONT

                def h(ch, e, p):
                    dve.wait_ge(silu_done, ch * ITEMS + e + 1)
                    dve.wait_ge(yd_ready, ch * ITEMS + e - 1 + 2)
                    nc.vector.tensor_tensor(hh[:, e % 2], sg[:, e % 2], gu[:, p % 2, 1], ALU.mult).then_inc(h_ready, 1)

                def add_y(ch, e, s):
                    dve.wait_ge(yd_ready, ch * ITEMS + e + 1 + 2)
                    for j in range(TJ):
                        if e < EXPERTS:
                            last = nc.vector.scalar_tensor_tensor(ysum[:, j], yd[:, e % 2, j], comb[:, s, j, e:e + 1], ysum[:, j], ALU.mult, ALU.add)
                        else:
                            last = nc.vector.tensor_tensor(ysum[:, j], yd[:, e % 2, j], ysum[:, j], ALU.add)
                    last.then_inc(yd_free, 1)
                    dve.wait_ge(yd_free, ch * ITEMS + e + 1 + 2)

                def chunk(ch, b, cc, s, nxt):
                    base = ch * PER + FRONT
                    for e in range(ITEMS):
                        p = place(e) if nxt else e
                        h(ch, e, p)
                        if e == 0:
                            dve.wait_ge(x1_ready, ch + 1)
                            for j in range(TJ):
                                last = nc.vector.scalar_tensor_tensor(ysum[:, j], x1[:, s, j], comb[:, s, j, EXPERTS:EXPERTS + 1], x1[:, s, j],
                                                                      ALU.mult, ALU.add)
                            last.then_inc(seq, 1)
                            dve.wait_ge(seq, base + 1)
                        else:
                            add_y(ch, e - 1, s)
                        if nxt:
                            nb, ncc = (b, cc + 1) if cc < CPB - 1 else (b + 1, 0)
                            if e == 3:
                                front_a(ch + 1, nb, ncc, 1 - s, base + 1)
                            if e == 5:
                                front_b(ch + 1, 1 - s, base + 1)
                            if e == ROUTE_AFTER:
                                front_c(ch + 1, 1 - s, base + 1, FIRST + ch * RING + ROUTE, ROUTE % 2)
                            if e == 12:
                                front_d(ch + 1, 1 - s, base + 1)
                    add_y(ch, ITEMS - 1, s)
                    after = base + 1 + (FRONT if nxt else 0)
                    variance(ysum[:], 1, after + 1).then_inc(var2, 1)
                    dve.wait_ge(std2, ch + 1)
                    dve.wait_ge(y_out[s], (b * 2 + cc // 2 + 1) * 16)
                    normalise(y[:, s], ysum[:], 1, after + 2).then_inc(y_ready, 1)
                    dve.wait_ge(y_ready, ch + 1)

                front_a(0, 0, 0, 0, 0)
                front_b(0, 0, 0)
                front_c(0, 0, 0, 1, 1)
                front_d(0, 0, 0)
                with dve.Fori(0, BATCH - 1) as b:
                    for cc in range(CPB):
                        chunk(b * CPB + cc, b, cc, cc % 2, True)
                for cc in range(CPB):
                    chunk(NCHUNK - CPB + cc, BATCH - 1, cc, cc % 2, cc < CPB - 1)

            @block.tensor
            def _(pe):
                pe.sem_inc(yd_ready, 2)
                pe.wait_ge(w_in, 16 * 8)
                pe.wait_ge(consts, 5)

                def front_turn(ch, s, slot):
                    pe.wait_ge(x1_ready, ch + 1)
                    for a in range(HALVES):
                        for j in range(TJ):
                            last = nc.tensor.transpose(gu[:, slot, a, j * P:(j + 1) * P], x1[:, s, j, a * P:(a + 1) * P], identity[:])
                    last.then_inc(gu_ready, 1)

                def front_route(ch, s, slot):
                    pe.wait_ge(xt_ready, ch + 1)
                    for j in range(TJ):
                        o = gu[:, slot, 0, j * HEADS:(j + 1) * HEADS]
                        for a in range(HALVES):
                            c0 = TAPS - 1 + j * P
                            nc.tensor.matmul(o, xT[:, s, a, c0:c0 + P], router_w[:, a], start=(a == 0), stop=False)
                        last = nc.tensor.matmul(o, ones[:], router_b[:], start=False, stop=True)
                    last.then_inc(gu_ready, 1)

                def item_read(ch, e):
                    pe.wait_ge(h_ready, ch * ITEMS + e + 1 + 2)

                def up(ch, s, e, p, nxt):
                    if nxt and p - 2 == TURN:
                        pe.wait_ge(xt_ready, ch + 2)
                    elif nxt and p - 2 == ROUTE:
                        pe.wait_ge(logit_ready, ch + 2)
                    else:
                        item_read(ch, e - 1 if nxt and p - 1 in (TURN, ROUTE) else e - 2)
                    if e == 0:
                        pe.wait_ge(logit_ready, ch + 1)
                    g, u = gu[:, p % 2, 0], gu[:, p % 2, 1]
                    now = slice(TAPS - 1, TAPS - 1 + CHUNK)
                    if e < EXPERTS:
                        for a in range(HALVES):
                            nc.tensor.matmul(g, gate_w[:, e, a], xT[:, s, a, now], start=(a == 0), stop=(a == 1))
                        for a in range(HALVES):
                            last = nc.tensor.matmul(u, up_w[:, e, a], xT[:, s, a, now], start=(a == 0), stop=(a == 1))
                    else:
                        for k in range(TAPS):
                            for a in range(HALVES):
                                nc.tensor.matmul(g, conv_w[:, k, a], xT[:, s, a, k:k + CHUNK], start=(k + a == 0),
                                                 stop=(k == TAPS - 1 and a == 1))
                        for a in range(HALVES):
                            last = nc.tensor.matmul(u, sup_w[:, a], xT[:, s, a, now], start=(a == 0), stop=(a == 1))
                    last.then_inc(gu_ready, 1)

                def down(ch, e):
                    pe.wait_ge(h_ready, ch * ITEMS + e + 1 + 2)
                    pe.wait_ge(yd_free, ch * ITEMS + e + 1)
                    w = down_w[:, e] if e < EXPERTS else sdown_w[:]
                    for j in range(TJ):
                        last = nc.tensor.matmul(yd[:, e % 2, j], hh[:, e % 2, j * P:(j + 1) * P], w, start=True, stop=True)
                    last.then_inc(yd_ready, 1)

                def chunk(ch, s, nxt):
                    for e in range(ITEMS):
                        p = place(e) if nxt else e
                        up(ch, s, e, p, nxt)
                        if e:
                            down(ch, e - 1)
                        if nxt and e == TURN_AFTER:
                            item_read(ch, TURN_AFTER - 1)
                            front_turn(ch + 1, 1 - s, TURN % 2)
                        if nxt and e == ROUTE_AFTER:
                            item_read(ch, ROUTE_AFTER - 1)
                            front_route(ch + 1, 1 - s, ROUTE % 2)
                    down(ch, ITEMS - 1)

                front_turn(0, 0, 0)
                front_route(0, 0, 1)
                with pe.Fori(0, BATCH - 1) as b:
                    for cc in range(CPB):
                        chunk(b * CPB + cc, cc % 2, True)
                for cc in range(CPB):
                    chunk(NCHUNK - CPB + cc, cc % 2, cc < CPB - 1)


def scratch(nc):
    def dram(name, shape, dt=F32):
        return nc.dram_tensor(name, shape, dt).ap()

    return {
        "q": dram("s_q", [3, NH * HD, SEQ], BF16),
        "k": dram("s_k", [3, NH * HD, SEQ], BF16),
        "v": dram("s_v", [NH, P, KT, VW]),
        "vlow": dram("s_vlow", [NH, NBLK, VW]),
        "low": dram("s_low", [NH, NBLK, NBLK]),
        "lowm": dram("s_lowm", [NH, NBLK, NBLK]),
        "mask": dram("s_mask", [NH, NBLK, NBLK], BF16),
        "rm": dram("s_rm", [4, NH, KT]),
    }


_IN = {
    "xt": [NCHUNK, P, HALVES, CHUNK], "x": [BATCH * SEQ, D],
    "wq": [P, HALVES, D], "wk": [P, HALVES, D], "wv": [P, HALVES, D],
    "bias_qk": [P, 2, HALVES], "bias_head": [HD, 2, HEADS], "bv": [1, D],
    "router": [P, HALVES, HEADS], "router_bias": [1, HEADS],
    "gate": [P, EXPERTS, HALVES, INNER], "up": [P, EXPERTS, HALVES, INNER], "down": [INNER, EXPERTS, D],
    "conv": [P, TAPS, HALVES, INNER], "shared_up": [P, HALVES, INNER], "shared_down": [INNER, D],
}


def build(nc, t, out):
    scr = scratch(nc)
    prepare(nc, t, scr)
    with ExitStack() as ctx:
        att = ctx.enter_context(nc.sbuf_tensor("att", [P, NH, KT, HD], F32))
        attend(nc, t, scr, att)
        ffn(nc, t, att, out)


def kernel(L0_attn_X, L0_attn_Wq, L0_attn_bq, L0_attn_Wk, L0_attn_bk, L0_attn_Wv, L0_attn_bv, L0_ffn_router_w,
           L0_ffn_router_bias, L0_ffn_expert_gate_w, L0_ffn_expert_up_w, L0_ffn_expert_down_w, L0_ffn_conv_w,
           L0_ffn_shared_up_w, L0_ffn_shared_down_w):
    import numpy as np
    import concourse.bacc as bacc
    from concourse.bass_utils import run_bass_kernel_spmd

    def rows(w):
        return np.asarray(w).reshape(HALVES, P, -1).transpose(1, 0, 2)

    def experts(w):
        return np.asarray(w).reshape(EXPERTS, HALVES, P, INNER).transpose(2, 0, 1, 3)

    x, bq, bk = (np.asarray(a) for a in (L0_attn_X, L0_attn_bq, L0_attn_bk))
    arrays = {
        "xt": x.reshape(NCHUNK, CHUNK, HALVES, P).transpose(0, 3, 2, 1),
        "x": x.reshape(BATCH * SEQ, D),
        "wq": rows(np.asarray(L0_attn_Wq).T), "wk": rows(np.asarray(L0_attn_Wk).T), "wv": rows(np.asarray(L0_attn_Wv).T),
        "bias_qk": np.stack([bq.reshape(HALVES, P).T, bk.reshape(HALVES, P).T], axis=1),
        "bias_head": np.stack([bq.reshape(HEADS, HD).T, bk.reshape(HEADS, HD).T], axis=1),
        "bv": np.asarray(L0_attn_bv).reshape(1, D),
        "router": rows(L0_ffn_router_w), "router_bias": np.asarray(L0_ffn_router_bias).reshape(1, HEADS),
        "gate": experts(L0_ffn_expert_gate_w), "up": experts(L0_ffn_expert_up_w),
        "down": np.asarray(L0_ffn_expert_down_w).transpose(1, 0, 2),
        "conv": np.asarray(L0_ffn_conv_w).transpose(2, 1, 0).reshape(TAPS, HALVES, P, INNER).transpose(2, 0, 1, 3),
        "shared_up": rows(L0_ffn_shared_up_w), "shared_down": np.asarray(L0_ffn_shared_down_w),
    }
    arrays = {"in_" + n: np.ascontiguousarray(a) for n, a in arrays.items()}
    nc = bacc.Bacc("TRN2", target_bir_lowering=False, num_devices=1)
    t = {n: nc.dram_tensor("in_" + n, shape, F32, kind="ExternalInput").ap() for n, shape in _IN.items()}
    out = nc.dram_tensor("out", [BATCH * SEQ, D], F32, kind="ExternalOutput").ap()
    build(nc, t, out)
    r = run_bass_kernel_spmd(nc, [arrays], core_ids=[0])
    return r.results[0]["out"].reshape(BATCH, SEQ, D)
```

```python
from contextlib import ExitStack

import concourse.bass as bass
from concourse import mybir

ALU = mybir.AluOpType
ACT = mybir.ActivationFunctionType
F32 = mybir.dt.float32
BF16 = mybir.dt.bfloat16
AX_X = mybir.AxisListType.X
ds = bass.ds

P = 128
BATCH, SEQ, D = 4, 2048, 256
HEADS, HD = 16, 16
BLK = 32
NBLK = SEQ // BLK
PAIRS = 1024 // BLK * 8
NH = BATCH * HEADS
HALVES = D // P
CHUNK = 512
CPB = SEQ // CHUNK
NCHUNK = BATCH * CPB
SCALE = 0.25
BIG = 1e9
VW = 32
KT = SEQ // P
UNITS = (KT + 1) * CPB
GRP = NBLK // 2
EXPERTS, INNER, TAPS = 15, 128, 3
EPS_LN, EPS_DEN = 1e-5, 1e-6


def prepare(nc, t, scr):
    with ExitStack() as ctx:
        def sb(name, shape, dt=F32):
            return ctx.enter_context(nc.sbuf_tensor(name, shape, dt))

        def sem(name):
            return ctx.enter_context(nc.semaphore(name))

        XSLOTS = 4
        xt = sb("xt", [P, XSLOTS, HALVES, CHUNK])
        wq, wk, wv = (sb(n, [P, HALVES, D]) for n in ("wq", "wk", "wv"))
        bias_qk = sb("bias_qk", [P, 2, HALVES])
        bias_q = sb("bias_q", [P, HALVES])
        bias_head = sb("bias_head", [HD, 2, HEADS])
        bv_row = sb("bv_row", [1, D])
        ones_row = sb("ones_row", [1, P])
        blk_row = sb("blk_row", [1, NBLK])
        xsum = sb("xsum", [P, HALVES, BATCH * NBLK])
        qh = sb("qh", [HD, 2, HEADS, BATCH * NBLK])
        lows = sb("lows", [NBLK, NH * NBLK])
        x32 = sb("x32", [P, 2, CHUNK])
        parts = sb("parts", [P, 4, 3, CHUNK], BF16)
        vs = sb("vs", [P, 2, HEADS, 4, VW])
        vlow = sb("vlow", [NBLK, NH, VW])
        low = sb("low", [NH, NBLK * NBLK])
        norm = sb("norm", [NH, NBLK * NBLK])
        work = sb("work", [NH, NBLK * NBLK])
        maskb = sb("maskb", [NH, NBLK * NBLK], BF16)
        rm = sb("rm", [NH, NBLK])
        rm4 = sb("rm4", [NH, 4, KT])
        st = sb("st", [NH, 16])
        ge = lows

        ps_qk = ctx.enter_context(nc.psum_tensor("ps_qk", [P, 4, CHUNK], F32))
        ps_v = ctx.enter_context(nc.psum_tensor("ps_v", [P, 2, CHUNK], F32))
        ps_m = ctx.enter_context(nc.psum_tensor("ps_m", [P, 2, CHUNK], F32))

        w_in = sem("w_in")
        xt_in = [sem(f"xt_in{k}") for k in range(XSLOTS)]
        bias_ready = sem("bias_ready")
        rows_set, blocks_summed = sem("rows_set"), sem("blocks_summed")
        m_ready, m_free = sem("m_ready"), sem("m_free")
        qk_ready, x_ready = sem("qk_ready"), sem("x_ready")
        r1_done, p2_done, p3_done = sem("r1_done"), sem("p2_done"), sem("p3_done")
        parts_stored = [sem(f"parts_stored{u}") for u in range(4)]
        v_ready, v_packed, v_pad = sem("v_ready"), sem("v_packed"), sem("v_pad")
        v_stored = [sem(f"v_stored{u}") for u in range(2)]
        low_stored, low_in, sel = sem("low_stored"), sem("low_in"), sem("sel")
        masks_ready, out_stored = sem("masks_ready"), sem("out_stored")

        MU = 16
        LU = 8

        with nc.Block() as block:
            @block.sync
            def _(sp):
                for dst, src in ((wq, t["wq"]), (wk, t["wk"]), (wv, t["wv"]), (bias_qk, t["bias_qk"]),
                                 (bias_head, t["bias_head"]), (bv_row, t["bv"])):
                    sp.dma_start(dst[:], src).then_inc(w_in, 16)
                for k in range(NCHUNK):
                    if k >= XSLOTS:
                        sp.wait_ge(blocks_summed, k - XSLOTS + 1)
                    sp.dma_start(xt[:, k % XSLOTS], t["xt"][k]).then_inc(xt_in[k % XSLOTS], 16)
                sp.wait_ge(blocks_summed, NCHUNK)
                for k in range(XSLOTS):
                    sp.dma_start(xt[:, k], t["xt"][k]).then_inc(xt_in[k], 16)
                sp.wait_ge(m_free, 2 + MU + LU)
                sp.dma_start(scr["low"].rearrange("n q k -> q n k"),
                             lows[:].rearrange("q (n k) -> q n k", n=NH)).then_inc(low_stored, 16)
                sp.wait_ge(low_stored, 16)
                sp.dma_start(low[:], scr["low"].rearrange("n q k -> n (q k)")).then_inc(low_in, 16)

                def store_chunk(b, cc):
                    for u in range(4):
                        sp.wait_ge(p3_done, (b * CPB + cc) * 4 + u + 1 + 2)
                        dst = scr["q"] if u < 2 else scr["k"]
                        sp.dma_start(
                            dst[:, ds(b * D + (u % 2) * P, P), cc * CHUNK:(cc + 1) * CHUNK].rearrange("s p t -> p s t"),
                            parts[:, u]).then_inc(parts_stored[u], 16)
                    sp.wait_ge(v_packed, (b * CPB + cc + 1) * 2 + 2)
                    sp.dma_start(
                        scr["v"][ds(b * HEADS, HEADS), :, cc * 4:cc * 4 + 4].rearrange("h p t d -> p h (t d)"),
                        vs[:, cc % 2].rearrange("p h t d -> p h (t d)")).then_inc(v_stored[cc % 2], 16)

                with sp.Fori(0, BATCH - 1) as b:
                    for cc in range(CPB):
                        store_chunk(b, cc)
                        sp.wait_ge(v_ready, (b * CPB + cc + 1) * 2)
                        sp.dma_start(xt[:, cc], t["xt"][ds(b * CPB + cc + CPB, 1)].rearrange("o p a t -> (o p) a t"))\
                            .then_inc(xt_in[cc], 16)
                for cc in range(CPB):
                    store_chunk(BATCH - 1, cc)
                sp.wait_ge(m_free, 2 + MU + LU + BATCH)
                sp.dma_start(scr["vlow"].rearrange("n m d -> m n d"), vlow[:]).then_inc(out_stored, 16)
                sp.wait_ge(masks_ready, 1)
                sp.dma_start(scr["mask"].rearrange("n q k -> n (q k)"), maskb[:]).then_inc(out_stored, 16)
                sp.dma_start(scr["lowm"].rearrange("n q k -> n (q k)"), low[:]).then_inc(out_stored, 16)
                sp.dma_start(scr["rm"].rearrange("a n t -> n a t"), rm4[:]).then_inc(out_stored, 16)
                sp.wait_ge(out_stored, 16 * 4)
                for u in range(4):
                    sp.wait_ge(parts_stored[u], 16 * (NCHUNK + 1))
                for u in range(2):
                    sp.wait_ge(v_stored[u], 16 * (NCHUNK // 2 + 1))

            @block.gpsimd
            def _(pool):
                pool.sem_inc(p3_done, 2)
                nc.gpsimd.memset(ones_row[:], 1.0).then_inc(rows_set, 1)
                nc.gpsimd.memset(blk_row[:], float(BLK)).then_inc(rows_set, 1)
                nc.gpsimd.memset(vs[:], 0.0).then_inc(v_pad, 1)
                nc.gpsimd.memset(vlow[:], 0.0).then_inc(v_pad, 1)
                pool.wait_ge(v_pad, 2)
                nc.gpsimd.memset(vs[:, :, :, :, HD:HD + 1], 1.0).then_inc(v_pad, 1)
                nc.gpsimd.memset(vlow[:, :, HD:HD + 1], float(BLK)).then_inc(v_pad, 1)
                with pool.Fori(0, NCHUNK) as it:
                    for u in range(4):
                        n = it * 4 + u
                        xs = x32[:, u % 2]
                        pool.wait_ge(x_ready, n + 1 + 4)
                        nc.gpsimd.tensor_tensor(xs, xs, parts[:, u, 0], ALU.subtract).then_inc(r1_done, 1)
                        pool.wait_ge(p2_done, n + 1)
                        nc.gpsimd.tensor_tensor(parts[:, u, 2], xs, parts[:, u, 1], ALU.subtract).then_inc(p3_done, 1)

            @block.scalar
            def _(act):
                act.sem_inc(m_free, 2)
                act.sem_inc(x_ready, 4)
                act.sem_inc(v_packed, 2)
                for u in range(4):
                    act.sem_inc(parts_stored[u], 16)
                for u in range(2):
                    act.sem_inc(v_stored[u], 16)
                act.wait_ge(w_in, 16 * 6)
                nc.scalar.activation(bias_q[:], bias_qk[:, 0], ACT.Copy, scale=SCALE).then_inc(bias_ready, 1)
                act.wait_ge(bias_ready, 1)
                for u in range(MU):
                    act.wait_ge(m_ready, u + 1)
                    for i in range(2):
                        h = (u % 8) * 2 + i
                        last = nc.scalar.activation(qh[:, u // 8, h], ps_m[0:HD, u % 2, i * 256:(i + 1) * 256],
                                                    ACT.Identity, bias=bias_head[:, u // 8, h:h + 1], scale=1.0 / BLK)
                    last.then_inc(m_free, 1)
                for g in range(LU):
                    act.wait_ge(m_ready, MU + g + 1)
                    nc.scalar.activation(lows[:, g * 512:(g + 1) * 512], ps_m[0:NBLK, g % 2], ACT.Copy,
                                         scale=SCALE).then_inc(m_free, 1)
                act.wait_ge(v_pad, 4)
                for b in range(BATCH):
                    act.wait_ge(m_ready, MU + LU + b + 1)
                    nc.scalar.activation(vlow[:, b * HEADS:(b + 1) * HEADS, 0:HD],
                                         ps_m[0:NBLK, b % 2, 0:D].rearrange("p (h d) -> p h d", h=HEADS),
                                         ACT.Copy).then_inc(m_free, 1)

                def second_part(n, u):
                    act.wait_ge(r1_done, n + 1)
                    nc.scalar.activation(parts[:, u, 1], x32[:, u % 2], ACT.Copy).then_inc(p2_done, 1)

                with act.Fori(0, BATCH) as b:
                    for cc in range(CPB):
                        it = b * CPB + cc
                        for u in range(4):
                            n = it * 4 + u
                            act.wait_ge(qk_ready, n + 1)
                            act.wait_ge(parts_stored[u], (it + 1) * 16)
                            act.wait_ge(p3_done, n + 1)
                            bias, scale = (bias_q[:, u:u + 1], SCALE) if u < 2 else (bias_qk[:, 1, u - 2:u - 1], 1.0)
                            nc.scalar.activation(x32[:, u % 2], ps_qk[:, u], ACT.Identity, bias=bias, scale=scale)
                            nc.scalar.activation(parts[:, u, 0], ps_qk[:, u], ACT.Identity, bias=bias, scale=scale).then_inc(x_ready, 1)
                            if u:
                                second_part(n - 1, u - 1)
                        second_part(it * 4 + 3, 3)
                        act.wait_ge(v_stored[cc % 2], (b * 2 + cc // 2 + 1) * 16)
                        for j in range(2):
                            act.wait_ge(v_ready, it * 2 + j + 1)
                            nc.scalar.activation(
                                vs[:, cc % 2, :, 2 * j:2 * j + 2, 0:HD].rearrange("p h j d -> p j h d"),
                                ps_v[:, j].rearrange("p (j h d) -> p j h d", j=2, h=HEADS), ACT.Copy).then_inc(v_packed, 1)

            @block.vector
            def _(dve):
                for k in range(NCHUNK):
                    dve.wait_ge(xt_in[k % XSLOTS], 16 * (k // XSLOTS + 1))
                    nc.vector.reduce_sum(xsum[:, :, k * 16:(k + 1) * 16],
                                         xt[:, k % XSLOTS].rearrange("p a (n t) -> p a n t", t=BLK),
                                         AX_X).then_inc(blocks_summed, 1)
                steps = [0]

                def step(ins):
                    steps[0] += 1
                    ins.then_inc(sel, 1)
                    dve.wait_ge(sel, steps[0])

                T, U, SG, POS, V, CNT, C, K0, TH, NGE, NEQ, NEED, F, UJ, B2 = (st[:, i:i + 1] for i in range(15))
                dve.wait_ge(low_in, 16)
                low3 = low[:].rearrange("n (q k) -> n q k", q=NBLK)
                norm3 = norm[:].rearrange("n (q k) -> n q k", q=NBLK)
                step(nc.vector.reduce_max(rm[:], low3, AX_X))
                step(nc.vector.tensor_tensor(norm3, low3, rm[:].unsqueeze(2).to_broadcast([NH, NBLK, NBLK]), ALU.subtract))
                for s, n in ((0, NBLK), (1, NBLK - 1), (NBLK, NBLK - 1)):
                    d = norm[:, s:s + (NBLK + 1) * (n - 1) + 1:NBLK + 1]
                    step(nc.vector.tensor_scalar(d, d, 5000.0, None, ALU.add))

                def count(v, out):
                    return nc.vector.tensor_scalar(maskb[:], norm[:], v, 0.0, ALU.is_ge, ALU.add, accum_out=out)

                def holds():
                    step(count(V, CNT))
                    step(nc.vector.tensor_scalar(C, CNT, PAIRS - 0.5, POS, ALU.is_ge, ALU.is_equal))

                step(nc.vector.memset(V, 0.0))
                step(count(V, CNT))
                step(nc.vector.tensor_scalar(POS, CNT, PAIRS - 0.5, None, ALU.is_ge))
                step(nc.vector.tensor_scalar(SG, POS, 2.0, -1.0, ALU.mult, ALU.add))
                step(nc.vector.memset(T, 2.0 ** -126))
                step(nc.vector.tensor_scalar(V, T, SG, None, ALU.mult))
                holds()
                step(nc.vector.tensor_copy(K0, C))
                for e in (127, 64, 32, 16, 8, 4, 2, 1):
                    step(nc.vector.tensor_scalar(V, T, 2.0 ** e, SG, ALU.mult, ALU.mult))
                    holds()
                    step(nc.vector.tensor_scalar(F, C, 2.0 ** e - 1.0, 1.0, ALU.mult, ALU.add))
                    step(nc.vector.tensor_tensor(T, T, F, ALU.mult))
                step(nc.vector.tensor_copy(U, T))
                step(nc.vector.tensor_copy(UJ, T))
                base, per_bit = steps[0], 5
                with dve.Fori(0, 23) as j:
                    done = [0]

                    def turn(ins):
                        done[0] += 1
                        ins.then_inc(sel, 1)
                        dve.wait_ge(sel, base + j * per_bit + done[0])

                    turn(nc.vector.tensor_scalar(UJ, UJ, 0.5, None, ALU.mult))
                    turn(nc.vector.tensor_scalar(V, UJ, T, SG, ALU.add, ALU.mult))
                    turn(count(V, CNT))
                    turn(nc.vector.tensor_scalar(C, CNT, PAIRS - 0.5, POS, ALU.is_ge, ALU.is_equal))
                    turn(nc.vector.scalar_tensor_tensor(T, C, UJ, T, ALU.mult, ALU.add))
                steps[0] = base + 23 * per_bit
                step(nc.vector.tensor_scalar(F, U, 2.0 ** -23, K0, ALU.mult, ALU.mult))
                step(nc.vector.tensor_scalar(B2, F, T, -1.0, ALU.add, ALU.mult))
                step(nc.vector.tensor_tensor(V, T, K0, ALU.mult))
                step(nc.vector.tensor_tensor(V, V, POS, ALU.mult))
                step(nc.vector.tensor_scalar(F, POS, -1.0, 1.0, ALU.mult, ALU.add))
                step(nc.vector.tensor_tensor(B2, B2, F, ALU.mult))
                step(nc.vector.tensor_tensor(TH, V, B2, ALU.add))
                step(nc.vector.tensor_scalar(ge[:], norm[:], TH, 0.0, ALU.is_ge, ALU.add, accum_out=NGE))
                step(nc.vector.scalar_tensor_tensor(low[:], ge[:], -BIG, low[:], ALU.mult, ALU.add))
                step(nc.vector.tensor_scalar(norm[:], norm[:], TH, 0.0, ALU.is_equal, ALU.add, accum_out=NEQ))
                step(nc.vector.tensor_tensor(NEED, NEQ, NGE, ALU.subtract))
                step(nc.vector.tensor_scalar(NEED, NEED, float(PAIRS), None, ALU.add))
                step(nc.vector.tensor_tensor_scan(work[:], norm[:], norm[:], 0.0, ALU.add, ALU.max))
                step(nc.vector.scalar_tensor_tensor(work[:], work[:], NEED, norm[:], ALU.is_le, ALU.mult))
                step(nc.vector.tensor_tensor(work[:], work[:], norm[:], ALU.subtract))
                step(nc.vector.tensor_tensor(work[:], work[:], ge[:], ALU.add))
                step(nc.vector.tensor_copy(rm4[:], rm[:].rearrange("n (t a) -> n a t", a=4)))
                nc.vector.tensor_scalar(maskb[:], work[:], -1.0, BIG, ALU.add, ALU.mult).then_inc(masks_ready, 1)

            @block.tensor
            def _(pe):
                pe.wait_ge(w_in, 16 * 6)
                pe.wait_ge(rows_set, 2)
                pe.wait_ge(blocks_summed, NCHUNK)
                for u in range(MU):
                    pe.wait_ge(m_free, u + 1)
                    w = (wq, wk)[u // 8]
                    for i in range(2):
                        h = (u % 8) * 2 + i
                        for a in range(HALVES):
                            last = nc.tensor.matmul(ps_m[0:HD, u % 2, i * 256:(i + 1) * 256], w[:, a, h * HD:(h + 1) * HD],
                                                    xsum[:, a], start=(a == 0), stop=(a == HALVES - 1))
                    last.then_inc(m_ready, 1)
                pe.wait_ge(m_free, 2 + MU)
                for g in range(LU):
                    pe.wait_ge(m_free, MU + g + 1)
                    for i in range(8):
                        b, h = divmod(g * 8 + i, HEADS)
                        last = nc.tensor.matmul(ps_m[0:NBLK, g % 2, i * NBLK:(i + 1) * NBLK],
                                                qh[:, 0, h, b * NBLK:(b + 1) * NBLK], qh[:, 1, h, b * NBLK:(b + 1) * NBLK],
                                                start=True, stop=True)
                    last.then_inc(m_ready, 1)
                for b in range(BATCH):
                    pe.wait_ge(m_free, MU + LU + b + 1)
                    out = ps_m[0:NBLK, b % 2, 0:D]
                    for a in range(HALVES):
                        nc.tensor.matmul(out, xsum[:, a, b * NBLK:(b + 1) * NBLK], wv[:, a], start=(a == 0), stop=False)
                    nc.tensor.matmul(out, blk_row[:], bv_row[:], start=False, stop=True).then_inc(m_ready, 1)
                with pe.Fori(0, BATCH) as b:
                    for cc in range(CPB):
                        it = b * CPB + cc
                        pe.wait_ge(xt_in[cc], (b + 1 + NCHUNK // XSLOTS) * 16)
                        for u in range(4):
                            pe.wait_ge(x_ready, it * 4 + u + 1)
                            w = (wq, wk)[u // 2]
                            for a in range(HALVES):
                                last = nc.tensor.matmul(ps_qk[:, u], w[:, a, (u % 2) * P:(u % 2 + 1) * P], xt[:, cc, a],
                                                        start=(a == 0), stop=(a == HALVES - 1))
                            last.then_inc(qk_ready, 1)
                        for j in range(2):
                            pe.wait_ge(v_packed, it * 2 + j + 1)
                            for i in range(2):
                                out = ps_v[:, j, i * D:(i + 1) * D]
                                tok = slice((2 * j + i) * P, (2 * j + i + 1) * P)
                                for a in range(HALVES):
                                    nc.tensor.matmul(out, xt[:, cc, a, tok], wv[:, a], start=(a == 0), stop=False)
                                last = nc.tensor.matmul(out, ones_row[:], bv_row[:], start=False, stop=True)
                            last.then_inc(v_ready, 1)


def attend(nc, t, scr, att, early):
    with ExitStack() as ctx:
        def sb(name, shape, dt=F32):
            return ctx.enter_context(nc.sbuf_tensor(name, shape, dt))

        def sem(name):
            return ctx.enter_context(nc.semaphore(name))

        SLOTS = 3
        PTS = 8
        BODY = 6
        TURNS = (NH - 4) // BODY
        HALFK = SEQ // 2
        MASK = slice(2 * GRP, 3 * GRP)
        qa, qb, ka = (sb(n, [P, SLOTS, SEQ], BF16) for n in ("qa", "qb", "ka"))
        v = sb("v", [P, SLOTS, KT + 2, VW])
        lw = sb("lw", [3 * GRP, SLOTS, NBLK])
        mask_in = sb("mask_in", [NBLK, NH, NBLK], BF16)
        mta, mtb = (sb(n, [3 * GRP, NH, NBLK], BF16) for n in ("mta", "mtb"))
        spread = sb("spread", [3 * GRP, SEQ])
        onehot = sb("onehot", [GRP, SEQ], BF16)
        ident = sb("ident", [P, P], BF16)
        identf = sb("identf", [GRP, GRP])
        fold = sb("fold", [P, VW])
        rmx = sb("rmx", [P, NH * KT])
        mx = sb("mx", [P, SLOTS, KT, 3])
        mfull = sb("mfull", [P, SLOTS, KT])
        mb = sb("mb", [P, SLOTS, KT], BF16)
        md = sb("md", [P, SLOTS, KT])
        nothing = sb("nothing", [P, 4])
        me = sb("me", [P, SLOTS, KT])
        pt = sb("pt", [P, PTS, CHUNK])
        os_ = sb("os_", [P, 2, CHUNK])
        den = sb("den", [P, 2, CPB])

        s1 = ctx.enter_context(nc.psum_tensor("s1", [P, 2, HALFK], F32))
        s2 = ctx.enter_context(nc.psum_tensor("s2", [P, 2, CHUNK], F32))
        acc = ctx.enter_context(nc.psum_tensor("acc", [P, 2, CHUNK], F32))

        start_in, consts, const2 = sem("start_in"), sem("consts"), sem("const2")
        mt_ready, mt_done = sem("mt_ready"), sem("mt_done")
        head_in = [sem(f"head_in{k}") for k in range(SLOTS)]
        expanded = sem("expanded")
        shifted = sem("shifted")
        s1_ready, s1_free = sem("s1_ready"), sem("s1_free")
        low_copied, full_max, rounded, mb_ready = sem("low_copied"), sem("full_max"), sem("rounded"), sem("mb_ready")
        s2_ready, s2_free = sem("s2_ready"), sem("s2_free")
        pv_done = sem("pv_done")
        os_ready, o_ready, den_done, rec_done, acc_free = (sem(n) for n in ("os_ready", "o_ready", "den_done", "rec_done", "acc_free"))

        ROWS = 18
        HEAD_IN = 16 * (ROWS + 4)
        PV_FREE = PTS
        BPOS = (21, 37, 57)
        OWN = 5
        RING = UNITS + CPB
        TILES = 2 * KT

        FIRST = CPB - 1

        def pos(r, nxt):
            return r + (r > OWN) + (sum(x < r for x in BPOS) if nxt else 0)

        def bank2(p):
            return (FIRST + p) % 2

        def place(n, r):
            return (n * UNITS + r) % PTS

        per_unit = [0] * (UNITS + 1)
        per_unit[0] = per_unit[UNITS - 1] = 2
        for q in range(UNITS // 4 - 1):
            if q in (6, 10):
                per_unit[4 * q + 3] += 2
            else:
                ahead = 2 * (4 * q + 1 in (OWN, *BPOS))
                per_unit[4 * q + 2] += ahead
                per_unit[4 * q + 3] += 3 - ahead
                per_unit[4 * q + 4] += 1
        assert sum(per_unit) == 2 * TILES

        def pass1_products(r):
            return list(range(sum(per_unit[:r]), sum(per_unit[:r + 1])))

        def pass1_units(r):
            return [w // 2 for w in pass1_products(r) if w % 2]

        with nc.Block() as block:
            @block.sync
            def _(sp):
                for a in range(4):
                    src = scr["rm"][a].rearrange("n t -> (n t)").unsqueeze(0).to_broadcast([GRP, NH * KT])
                    sp.dma_start(rmx[a * GRP:(a + 1) * GRP], src).then_inc(start_in, 16)
                sp.dma_start(mask_in[:], scr["mask"].rearrange("n q k -> q n k")).then_inc(start_in, 16)

                def load(m, slot):
                    def rows(dst, at, src, part):
                        sp.dma_start(dst[at:at + HD, slot], src[part, ds(m * HD, HD)]).then_inc(head_in[slot], 16)

                    for at, pq, pk in ((0, 0, 0), (16, 0, 1), (32, 1, 0), (48, 1, 1), (96, 0, 2), (112, 2, 0)):
                        rows(qa, at, scr["q"], pq)
                        rows(qb, at, scr["q"], pq)
                        rows(ka, at, scr["k"], pk)
                    one = ds(m, 1)
                    sp.dma_start(v[:, slot, 0:KT], scr["v"][one].rearrange("o p t d -> (o p) t d")).then_inc(head_in[slot], 16)
                    for i in range(2):
                        sp.dma_start(v[i * NBLK:(i + 1) * NBLK, slot, KT + i],
                                     scr["vlow"][one].rearrange("o m d -> (o m) d")).then_inc(head_in[slot], 16)
                    sp.dma_start(lw[0:NBLK, slot], scr["lowm"][one].rearrange("o q k -> (o q) k")).then_inc(head_in[slot], 16)

                def load_after(n, slot):
                    sp.wait_ge(pv_done, n * UNITS + PV_FREE)
                    load(n + 2, slot)

                load(0, 0)
                load(1, 1)
                load(2, 2)
                for dst, name, done in early:
                    sp.dma_start(dst[:], t[name]).then_inc(done, 16)
                with sp.Fori(0, TURNS) as i:
                    for h in range(1, BODY + 1):
                        load_after(i * BODY + h, (h + 2) % SLOTS)
                load_after(NH - 3, (NH - 1) % SLOTS)

            @block.gpsimd
            def _(pool):
                nc.gpsimd.memset(ident[:], 0.0).then_inc(consts, 1)
                nc.gpsimd.memset(identf[:], 0.0).then_inc(consts, 1)
                nc.gpsimd.memset(spread[:], 0.0).then_inc(consts, 1)
                nc.gpsimd.memset(onehot[:], 0.0).then_inc(consts, 1)
                pool.wait_ge(consts, 4 + 1)

                def diagonal(ap, pattern):
                    return nc.gpsimd.affine_select(out=ap, in_=ap, compare_op=ALU.not_equal, fill=1.0, base=0,
                                                   pattern=pattern, channel_multiplier=1)

                diagonal(ident[:], [[-1, P]]).then_inc(const2, 1)
                diagonal(identf[:], [[-1, GRP]]).then_inc(const2, 1)
                diagonal(spread[0:NBLK].rearrange("p (b t) -> p b t", t=BLK), [[-1, NBLK], [0, BLK]]).then_inc(const2, 1)
                diagonal(onehot[:].rearrange("p (g b t) -> p g b t", g=2, t=BLK), [[0, 2], [-1, GRP], [0, BLK]]).then_inc(const2, 1)

                def expand(m, slot, half):
                    q, mt = ((qa, mta), (qb, mtb))[half]
                    one = mt[MASK, ds(m, 1)].rearrange("p o b -> p (o b)")
                    nc.gpsimd.tensor_copy(q[MASK, slot].rearrange("p (b t) -> p b t", t=BLK),
                                          one.unsqueeze(2).to_broadcast([GRP, NBLK, BLK])).then_inc(expanded, 1)

                def low_max(m, slot):
                    nc.gpsimd.tensor_copy(mx[:, slot, :, 2], rmx[:, ds(m * KT, KT)]).then_inc(low_copied, 1)
                    pool.wait_ge(low_copied, m + 1)

                def rounding(m, slot, c):
                    k, cols = m * CPB + c + 1, slice(c * 4, c * 4 + 4)
                    pool.wait_ge(full_max, k)
                    nc.gpsimd.tensor_tensor(mb[:, slot, cols], mfull[:, slot, cols], nothing[:], ALU.add).then_inc(rounded, 1)
                    pool.wait_ge(rounded, k)
                    nc.gpsimd.tensor_tensor(md[:, slot, cols], mfull[:, slot, cols], mb[:, slot, cols], ALU.subtract).then_inc(mb_ready, 1)

                def shift(m, slot, c, ring):
                    pool.wait_ge(s2_free, ring + 1 + 2)
                    for q in (qa, qb):
                        part = q[MASK, slot, c * CHUNK:(c + 1) * CHUNK]
                        last = nc.gpsimd.tensor_tensor(part, part, spread[MASK, c * CHUNK:(c + 1) * CHUNK], ALU.subtract)
                    last.then_inc(shifted, 1)

                pool.wait_ge(mt_done, 16)
                pool.wait_ge(const2, 8)
                pool.wait_ge(start_in, 16 * 5)
                low_max(0, 0)
                low_max(1, 1)
                for half in range(2):
                    expand(1, 1, half)
                pool.wait_ge(expanded, 4)
                for c in range(CPB - 1):
                    rounding(0, 0, c)
                    shift(0, 0, c, c)
                    pool.wait_ge(shifted, c + 1)
                rounding(0, 0, CPB - 1)

                def step(n, j, more):
                    shift(n, j, CPB - 1, FIRST + n * RING + OWN + 1)
                    pool.wait_ge(shifted, (n + 1) * CPB)
                    for c in range(CPB - 1):
                        rounding(n + 1, (j + 1) % SLOTS, c)
                        shift(n + 1, (j + 1) % SLOTS, c, FIRST + n * RING + BPOS[c] + 2 + c)
                        pool.wait_ge(shifted, (n + 1) * CPB + c + 1)
                        if more and c < 2:
                            pool.wait_ge(pv_done, n * UNITS + PV_FREE)
                            if c == 0:
                                low_max(n + 2, (j + 2) % SLOTS)
                            expand(n + 2, (j + 2) % SLOTS, c)
                            pool.wait_ge(expanded, 2 * (n + 2) + c + 1)
                    rounding(n + 1, (j + 1) % SLOTS, CPB - 1)

                step(0, 0, True)
                with pool.Fori(0, TURNS) as i:
                    for h in range(1, BODY + 1):
                        step(i * BODY + h, h % SLOTS, True)
                step(NH - 3, (NH - 3) % SLOTS, True)
                step(NH - 2, (NH - 2) % SLOTS, False)
                shift(NH - 1, (NH - 1) % SLOTS, CPB - 1, FIRST + (NH - 1) * RING + OWN + 1)

            @block.scalar
            def _(act):
                act.sem_inc(s2_free, 2)

                def shift(m, slot, c, ring, bank):
                    act.wait_ge(mb_ready, m * CPB + c + 1)
                    cols = slice(c * 4, c * 4 + 4)
                    nc.scalar.activation(me[:, slot, cols], md[:, slot, cols], ACT.Exp)
                    act.wait_ge(s2_ready, ring + 1)
                    nc.scalar.activation(spread[MASK, c * CHUNK:(c + 1) * CHUNK], s2[MASK, bank],
                                         ACT.Copy).then_inc(s2_free, 1)

                def evacuate(n, c):
                    act.wait_ge(pv_done, PV_FREE + n * UNITS + (c + 1) * (KT + 1))
                    nc.scalar.activation(os_[:, c % 2], acc[:, c % 2], ACT.Copy).then_inc(os_ready, 1)

                def step(n, j, par, nxt, before):
                    for r in range(UNITS):
                        c, k = divmod(r, KT + 1)
                        p = pos(r, nxt)
                        act.wait_ge(s2_ready, FIRST + n * RING + p + 1)
                        act.wait_ge(pv_done, n * UNITS + r + 1)
                        n_cols = CHUNK // 2 if k == KT else CHUNK
                        nc.scalar.activation(pt[:, place(par, r), 0:n_cols], s2[:, bank2(p), 0:n_cols], ACT.Exp).then_inc(s2_free, 1)
                        if r == OWN:
                            shift(n, j, CPB - 1, FIRST + n * RING + p + 1, bank2(p + 1))
                        if nxt and r in BPOS:
                            shift(n + 1, (j + 1) % SLOTS, BPOS.index(r), FIRST + n * RING + p + 1, bank2(p + 1))
                        if k == 5 and c:
                            evacuate(n, c - 1)
                        elif k == 5 and before:
                            evacuate(n - 1, CPB - 1)

                act.wait_ge(const2, 8)
                for c in range(CPB - 1):
                    shift(0, 0, c, c, c % 2)
                step(0, 0, 0, True, False)
                with act.Fori(0, TURNS) as i:
                    for h in range(1, BODY + 1):
                        step(i * BODY + h, h % SLOTS, h, True, True)
                for n in range(NH - 3, NH):
                    step(n, n % SLOTS, n, n < NH - 1, True)
                evacuate(NH - 1, CPB - 1)

            @block.vector
            def _(dve):
                dve.sem_inc(s1_free, 2)
                dve.sem_inc(acc_free, 2)
                nc.vector.memset(lw[MASK], 0.0).then_inc(consts, 1)
                nc.vector.memset(v[NBLK:P, :, KT], 0.0).then_inc(const2, 1)
                nc.vector.memset(v[0:NBLK, :, KT + 1], 0.0).then_inc(const2, 1)
                nc.vector.memset(nothing[:], 0.0).then_inc(const2, 1)
                dve.wait_ge(consts, 5)
                nc.vector.memset(lw[2 * GRP:2 * GRP + 1], -1.0).then_inc(const2, 1)
                for g in range(8):
                    dve.wait_ge(mt_ready, g + 1)
                    bank = s1[:].rearrange("p g (h c) -> p (g h) c", c=CHUNK)[:, g % 4]
                    for q, mt in enumerate((mta, mtb)):
                        nc.vector.tensor_copy(mt[MASK, g * 8:(g + 1) * 8].rearrange("p n b -> p (n b)"),
                                              bank[q * GRP:(q + 1) * GRP]).then_inc(mt_done, 1)
                    if g == 0:
                        dve.wait_ge(mt_done, 2)
                        for q, mt in ((qa, mta), (qb, mtb)):
                            nc.vector.tensor_copy(q[MASK, 0].rearrange("p (b t) -> p b t", t=BLK),
                                                  mt[MASK, 0].unsqueeze(2).to_broadcast([GRP, NBLK, BLK])).then_inc(expanded, 1)
                dve.wait_ge(const2, 8)
                for k in range(SLOTS):
                    nc.vector.tensor_copy(ka[MASK, k], onehot[:])
                for a in range(4):
                    last = nc.vector.tensor_copy(fold[a * GRP:(a + 1) * GRP], identf[:])
                last.then_inc(consts, 1)

                def row_max(m, slot, u):
                    dve.wait_ge(s1_ready, m * TILES + u + 1)
                    nc.vector.reduce_max(mx[:, slot, u // 2, u % 2:u % 2 + 1], s1[:, u % 2], AX_X).then_inc(s1_free, 1)
                    if u % 8 == 7:
                        cols = slice(u // 8 * 4, u // 8 * 4 + 4)
                        dve.wait_ge(s1_free, m * TILES + u + 1 + 2)
                        nc.vector.reduce_max(mfull[:, slot, cols], mx[:, slot, cols], AX_X).then_inc(full_max, 1)

                def normalise(n, slot, c, part):
                    k, cols = n * CPB + c + 1, slice(c * 4, c * 4 + 4)
                    o = acc[:, c % 2, 0:4 * VW].rearrange("p (j d) -> p j d", d=VW)
                    if part == 0:
                        dve.wait_ge(o_ready, k)
                        nc.vector.scalar_tensor_tensor(den[:, 0], me[:, slot, cols], EPS_DEN,
                                                       o[:, :, HD:HD + 1].rearrange("p j d -> p (j d)"), ALU.mult, ALU.add).then_inc(den_done, 1)
                    elif part == 1:
                        dve.wait_ge(den_done, k)
                        nc.vector.reciprocal(den[:, 1], den[:, 0]).then_inc(rec_done, 1)
                    else:
                        dve.wait_ge(rec_done, k)
                        dst = att[:, ds(n, 1), cols].rearrange("p o j d -> p (o j) d")
                        nc.vector.tensor_tensor(dst, o[:, :, 0:HD], den[:, 1].unsqueeze(2).to_broadcast([P, 4, HD]), ALU.mult).then_inc(acc_free, 1)

                def step(n, j, nxt, before):
                    for r in range(UNITS):
                        c, k = divmod(r, KT + 1)
                        if nxt:
                            for u in pass1_units(r):
                                row_max(n + 1, (j + 1) % SLOTS, u)
                        if k in (12, 14, 16) and c:
                            normalise(n, j, c - 1, (k - 12) // 2)
                        elif k in (12, 14, 16) and before:
                            normalise(n - 1, (j - 1) % SLOTS, CPB - 1, (k - 12) // 2)

                dve.wait_ge(low_copied, 1)
                for u in range(TILES):
                    row_max(0, 0, u)
                step(0, 0, True, False)
                with dve.Fori(0, TURNS) as i:
                    for h in range(1, BODY + 1):
                        step(i * BODY + h, h % SLOTS, True, True)
                for n in range(NH - 3, NH):
                    step(n, n % SLOTS, n < NH - 1, True)
                for part in range(3):
                    normalise(NH - 1, (NH - 1) % SLOTS, CPB - 1, part)

            @block.tensor
            def _(pe):
                pe.sem_inc(pv_done, PV_FREE)
                pe.wait_ge(const2, 8)
                pe.wait_ge(start_in, 16 * 5)
                for g in range(8):
                    if g >= 4:
                        pe.wait_ge(mt_done, 2 * (g - 3))
                    bank = s1[:].rearrange("p g (h c) -> p (g h) c", c=CHUNK)[:, g % 4]
                    for i in range(8):
                        last = nc.tensor.matmul(bank[0:NBLK, i * NBLK:(i + 1) * NBLK], mask_in[:, g * 8 + i],
                                                ident[0:NBLK, 0:NBLK], start=True, stop=True)
                    last.then_inc(mt_ready, 1)
                pe.wait_ge(mt_done, 16)
                pe.wait_ge(consts, 6)

                def product1(m, slot, w):
                    u, i = divmod(w, 2)
                    tq, g = divmod(u, 2)
                    if i == 0:
                        pe.wait_ge(s1_free, m * TILES + u + 1)
                    k0 = g * HALFK + i * CHUNK
                    mm = nc.tensor.matmul(s1[:, g, i * CHUNK:(i + 1) * CHUNK], (qa, qb)[g][:, slot, tq * P:(tq + 1) * P],
                                          ka[:, slot, k0:k0 + CHUNK], start=True, stop=True)
                    if i == 1:
                        mm.then_inc(s1_ready, 1)

                def tile2(n, slot, r, p):
                    c, k = divmod(r, KT + 1)
                    cols = slice(c * CHUNK, (c + 1) * CHUNK)
                    if k == 0:
                        pe.wait_ge(shifted, n * CPB + c + 1)
                    pe.wait_ge(s2_free, FIRST + n * RING + p + 1)
                    if k == KT:
                        for i in range(2):
                            part = slice(c * CHUNK + i * (CHUNK // 2), c * CHUNK + (i + 1) * (CHUNK // 2))
                            mm = nc.tensor.matmul(s2[i * NBLK:(i + 1) * NBLK, bank2(p), 0:CHUNK // 2], lw[:, slot], spread[:, part],
                                                  start=True, stop=True)
                    else:
                        q = qa if k < KT // 2 else qb
                        mm = nc.tensor.matmul(s2[:, bank2(p)], ka[:, slot, k * P:(k + 1) * P], q[:, slot, cols], start=True, stop=True)
                    mm.then_inc(s2_ready, 1)

                def shift(m, slot, c, ring, bank):
                    pe.wait_ge(mb_ready, m * CPB + c + 1)
                    pe.wait_ge(s2_free, ring + 1)
                    for i in range(4):
                        tq = c * 4 + i
                        last = nc.tensor.matmul(s2[MASK, bank, i * P:(i + 1) * P], mb[:, slot, tq:tq + 1].to_broadcast([P, GRP]),
                                                ident[:], start=True, stop=True)
                    last.then_inc(s2_ready, 1)

                def times_v(n, slot, par, r, p):
                    c, k = divmod(r, KT + 1)
                    g = r % 4
                    pe.wait_ge(s2_free, FIRST + n * RING + p + 1 + 2)
                    if k == 0:
                        pe.wait_ge(acc_free, n * CPB + c + 1)
                    o = acc[g * VW:(g + 1) * VW, c % 2]
                    if k == KT:
                        for i in range(2):
                            mm = nc.tensor.matmul(o[:, i * (CHUNK // 2):(i + 1) * (CHUNK // 2)], v[:, slot, KT + i],
                                                  pt[:, place(par, r), 0:CHUNK // 2], start=False, stop=(i == 1))
                    else:
                        mm = nc.tensor.matmul(o, v[:, slot, k], pt[:, place(par, r)], start=(k < 4), stop=(k > KT - 4))
                    mm.then_inc(pv_done, 1)

                def fold_sums(n, c, i):
                    if i == 0:
                        pe.wait_ge(os_ready, n * CPB + c + 1)
                    mm = nc.tensor.matmul(acc[:, c % 2, i * VW:(i + 1) * VW], os_[:, c % 2, i * P:(i + 1) * P], fold[:],
                                          start=True, stop=True)
                    if i == 3:
                        mm.then_inc(o_ready, 1)

                def four_times_v(n, slot, par, q, nxt):
                    for r in range(4 * q, 4 * q + 4):
                        times_v(n, slot, par, r, pos(r, nxt))

                def step(n, j, par, nxt, before, turn=None):
                    if nxt:
                        pe.wait_ge(expanded, 2 * (n + 2))
                        pe.wait_ge(head_in[(j + 1) % SLOTS], turn * HEAD_IN)
                    for r in range(UNITS):
                        c, k = divmod(r, KT + 1)
                        p = pos(r, nxt)
                        tile2(n, j, r, p)
                        if nxt:
                            for w in pass1_products(r):
                                product1(n + 1, (j + 1) % SLOTS, w)
                        if r % 4 == 1:
                            if r > 1:
                                four_times_v(n, j, par, r // 4 - 1, nxt)
                            elif before:
                                four_times_v(n - 1, (j - 1) % SLOTS, par + 1, UNITS // 4 - 1, True)
                        if r == OWN:
                            shift(n, j, CPB - 1, FIRST + n * RING + p + 1, bank2(p + 1))
                        if nxt and r in BPOS:
                            shift(n + 1, (j + 1) % SLOTS, BPOS.index(r), FIRST + n * RING + p + 1, bank2(p + 1))
                        if 8 <= k < 12 and c:
                            fold_sums(n, c - 1, k - 8)
                        elif 8 <= k < 12 and before:
                            fold_sums(n - 1, CPB - 1, k - 8)

                pe.wait_ge(expanded, 2)
                pe.wait_ge(head_in[0], HEAD_IN)
                for w in range(2 * TILES):
                    product1(0, 0, w)
                for c in range(CPB - 1):
                    shift(0, 0, c, c, c % 2)
                step(0, 0, 0, True, False, 1)
                with pe.Fori(0, TURNS) as i:
                    for h in range(1, BODY + 1):
                        step(i * BODY + h, h % SLOTS, h, True, True, i * (BODY // SLOTS) + (h + 1) // SLOTS + 1)
                for n in range(NH - 3, NH):
                    step(n, n % SLOTS, n, n < NH - 1, True, (n + 1) // SLOTS + 1)
                four_times_v(NH - 1, (NH - 1) % SLOTS, NH - 1, UNITS // 4 - 1, False)
                for i in range(4):
                    fold_sums(NH - 1, CPB - 1, i)


def ffn(nc, t, att, out, gate_w, up_w, w_in):
    with ExitStack() as ctx:
        def sb(name, shape, dt=F32):
            return ctx.enter_context(nc.sbuf_tensor(name, shape, dt))

        def sem(name):
            return ctx.enter_context(nc.semaphore(name))

        TJ = CHUNK // P
        ITEMS = EXPERTS + 1
        RING = ITEMS + 2
        TURN_AFTER, ROUTE_AFTER = 8, 10
        down_w = sb("down_w", [INNER, EXPERTS, D])
        conv_w = sb("conv_w", [P, TAPS, HALVES, INNER])
        sup_w = sb("sup_w", [P, HALVES, INNER])
        sdown_w = sb("sdown_w", [INNER, D])
        router_w = sb("router_w", [P, HALVES, HEADS])
        router_b = sb("router_b", [1, HEADS])
        ones = sb("ones", [1, P])
        eps = sb("eps", [P, 1])
        zero = sb("zero", [P, HALVES, TAPS - 1])
        identity = sb("identity", [P, P])
        xin = sb("xin", [P, 2, TJ, D])
        x1 = sb("x1", [P, 2, TJ, D])
        xT = sb("xT", [P, 2, HALVES, TAPS - 1 + CHUNK])
        stats = sb("stats", [P, 2, TJ, 6])
        mv = sb("mv", [P, 2, TJ, 2])
        std = sb("std", [P, 2, TJ])
        rstd = sb("rstd", [P, 2, TJ])
        prob = sb("prob", [P, TJ, HEADS])
        comb = sb("comb", [P, 2, TJ, HEADS])
        gt, eq, rank = (sb(n, [P, TJ, HEADS]) for n in ("gt", "eq", "rank"))
        top = sb("top", [P, TJ, 8])
        col = sb("col", [P, 4, TJ])
        carrier = sb("carrier", [P, 1])
        sg = sb("sg", [P, 2, CHUNK])
        hh = sb("hh", [P, 2, CHUNK])
        ysum = sb("ysum", [P, TJ, D])
        y = sb("y", [P, 2, TJ, D])

        gu = ctx.enter_context(nc.psum_tensor("gu", [P, 2, 2, CHUNK], F32))
        yd = ctx.enter_context(nc.psum_tensor("yd", [P, 2, TJ, D], F32))

        consts = sem("ffn_consts")
        x_in = [sem(f"x_in{k}") for k in range(2)]
        y_out = [sem(f"y_out{k}") for k in range(2)]
        seq = sem("seq")
        gu_ready = sem("gu_ready")
        silu_done, h_ready, yd_ready, yd_free = (sem(n) for n in ("silu_done", "h_ready", "yd_ready", "yd_free"))
        var1, std1, var2, std2 = (sem(n) for n in ("var1", "std1", "var2", "std2"))
        x1_ready, xt_ready, logit_ready, exp_done = (sem(n) for n in ("x1_ready", "xt_ready", "logit_ready", "exp_done"))
        y_ready = sem("y_ready")

        def place(e):
            return e + (e > TURN_AFTER) + (e > ROUTE_AFTER)

        TURN, ROUTE = place(TURN_AFTER) + 1, place(ROUTE_AFTER) + 1
        FIRST = 2
        FRONT, TAIL = 16, 3
        PER = FRONT + TAIL

        with nc.Block() as block:
            @block.sync
            def _(sp):
                def tokens(ap, ch):
                    return ap[ds(ch * CHUNK, CHUNK)].rearrange("(j p) d -> p j d", p=P)

                def load(ch, s):
                    sp.dma_start(xin[:, s], tokens(t["x"], ch)).then_inc(x_in[s], 16)

                def store(ch, s):
                    sp.wait_ge(y_ready, ch + 1)
                    sp.dma_start(tokens(out, ch), y[:, s]).then_inc(y_out[s], 16)

                load(0, 0)
                for dst, name in ((router_w, "router"), (router_b, "router_bias"),
                                  (down_w, "down"), (conv_w, "conv"), (sup_w, "shared_up"), (sdown_w, "shared_down")):
                    sp.dma_start(dst[:], t[name]).then_inc(w_in, 16)
                load(1, 1)
                with sp.Fori(0, BATCH - 1) as b:
                    for cc in range(CPB):
                        store(b * CPB + cc, cc % 2)
                        load(b * CPB + cc + 2, cc % 2)
                for cc in range(CPB):
                    store(NCHUNK - CPB + cc, cc % 2)
                    if cc < 2:
                        load(NCHUNK - CPB + cc + 2, cc % 2)
                for s in range(2):
                    sp.wait_ge(y_out[s], 16 * (NCHUNK // 2 + 1))

            @block.gpsimd
            def _(pool):
                nc.gpsimd.memset(identity[:], 0.0).then_inc(consts, 1)
                nc.gpsimd.memset(ones[:], 1.0).then_inc(consts, 1)
                nc.gpsimd.memset(eps[:], EPS_LN).then_inc(consts, 1)
                nc.gpsimd.memset(zero[:], 0.0).then_inc(consts, 1)
                pool.wait_ge(consts, 4)
                nc.gpsimd.affine_select(out=identity[:], in_=identity[:], compare_op=ALU.not_equal, fill=1.0, base=0,
                                        pattern=[[-1, P]], channel_multiplier=1).then_inc(consts, 1)

            @block.scalar
            def _(act):
                for k in range(2):
                    act.sem_inc(y_out[k], 16)
                act.wait_ge(consts, 5)

                def root(var, ready, done, count, s):
                    act.wait_ge(ready, count)
                    nc.scalar.activation(std[:, s], var, ACT.Sqrt, bias=eps[:, 0:1]).then_inc(done, 1)

                def front_ln(ch, s):
                    root(mv[:, 0, :, 1], var1, std1, ch + 1, 0)

                def front_turn(ch, s, first, ring, slot):
                    act.wait_ge(gu_ready, ring + 1)
                    before = zero[:] if first else xT[:, 1 - s, :, CHUNK:CHUNK + TAPS - 1]
                    nc.scalar.activation(xT[:, s, :, 0:TAPS - 1], before, ACT.Copy)
                    nc.scalar.activation(xT[:, s, :, TAPS - 1:], gu[:, slot], ACT.Copy).then_inc(xt_ready, 1)

                def front_exp(ch):
                    act.wait_ge(logit_ready, ch + 1)
                    nc.scalar.activation(prob[:], prob[:], ACT.Exp).then_inc(exp_done, 1)

                def chunk(ch, s, nxt, first_next):
                    for e in range(ITEMS):
                        p = place(e) if nxt else e
                        act.wait_ge(gu_ready, FIRST + ch * RING + p + 1)
                        act.wait_ge(h_ready, ch * ITEMS + e + 1)
                        nc.scalar.activation(sg[:, e % 2], gu[:, p % 2, 0], ACT.Silu).then_inc(silu_done, 1)
                        if nxt and e == 4:
                            front_ln(ch + 1, 1 - s)
                        if nxt and e == TURN_AFTER:
                            front_turn(ch + 1, 1 - s, first_next, FIRST + ch * RING + TURN, TURN % 2)
                        if nxt and e == ROUTE_AFTER:
                            front_exp(ch + 1)
                    root(mv[:, 1, :, 1], var2, std2, ch + 1, 1)

                front_ln(0, 0)
                front_turn(0, 0, True, 0, 0)
                front_exp(0)
                with act.Fori(0, BATCH - 1) as b:
                    for cc in range(CPB):
                        chunk(b * CPB + cc, cc % 2, True, cc == CPB - 1)
                for cc in range(CPB):
                    chunk(NCHUNK - CPB + cc, cc % 2, cc < CPB - 1, False)

            @block.vector
            def _(dve):
                dve.sem_inc(h_ready, 2)
                dve.sem_inc(yd_free, 2)

                def normalise(dst, src, which, seq_at):
                    nc.vector.reciprocal(rstd[:, which], std[:, which]).then_inc(seq, 1)
                    dve.wait_ge(seq, seq_at)
                    for j in range(TJ):
                        last = nc.vector.tensor_scalar(dst[:, j], src[:, j], mv[:, which, j, 0:1], rstd[:, which, j:j + 1],
                                                       ALU.subtract, ALU.mult)
                    return last

                def variance(src, which, seq_at):
                    for j in range(TJ):
                        last = nc.vector.bn_stats(stats[:, which, j], src[:, j])
                    last.then_inc(seq, 1)
                    dve.wait_ge(seq, seq_at)
                    nc.vector.memset(carrier[:], 0.0)
                    for j in range(TJ):
                        last = nc.vector.bn_aggr(mv[:, which, j], stats[:, which, j])
                    return last

                def front_a(ch, b, cc, s, base):
                    dve.wait_ge(x_in[s], (b * 2 + cc // 2 + 1) * 16)
                    a = att[:, ds(b * HEADS, HEADS), cc * TJ:(cc + 1) * TJ].rearrange("p h j d -> p j h d")
                    nc.vector.tensor_tensor(x1[:, s].rearrange("p j (h d) -> p j h d", h=HEADS),
                                            xin[:, s].rearrange("p j (h d) -> p j h d", h=HEADS), a, ALU.add).then_inc(seq, 1)
                    dve.wait_ge(seq, base + 1)
                    variance(x1[:, s], 0, base + 2).then_inc(var1, 1)

                def front_b(ch, s, base):
                    dve.wait_ge(std1, ch + 1)
                    normalise(x1[:, s], x1[:, s], 0, base + 3).then_inc(x1_ready, 1)

                def front_c(ch, s, base, ring, slot):
                    dve.wait_ge(gu_ready, ring + 1)
                    lg = gu[:, slot, 0, 0:TJ * HEADS].rearrange("p (j e) -> p j e", j=TJ)
                    nc.vector.reduce_max(col[:, 0], lg, AX_X).then_inc(seq, 1)
                    dve.wait_ge(seq, base + 4)
                    nc.vector.tensor_tensor(prob[:], lg, col[:, 0].unsqueeze(2).to_broadcast([P, TJ, HEADS]),
                                            ALU.subtract).then_inc(logit_ready, 1)

                def front_d(ch, s, base):
                    done = [4]

                    def step(ins):
                        done[0] += 1
                        ins.then_inc(seq, 1)
                        dve.wait_ge(seq, base + done[0])

                    def wide(c):
                        return c.unsqueeze(2).to_broadcast([P, TJ, HEADS])

                    dve.wait_ge(exp_done, ch + 1)
                    step(nc.vector.reduce_sum(col[:, 0], prob[:], AX_X))
                    step(nc.vector.reciprocal(col[:, 1], col[:, 0]))
                    step(nc.vector.tensor_tensor(prob[:], prob[:], wide(col[:, 1]), ALU.mult))
                    nc.vector.memset(carrier[:], 0.0)
                    for j in range(TJ):
                        last = nc.vector.max(top[:, j], prob[:, j])
                    step(last)
                    second = top[:, :, 1]
                    nc.vector.tensor_tensor(gt[:], prob[:], wide(second), ALU.is_gt)
                    nc.vector.tensor_tensor(eq[:], prob[:], wide(second), ALU.is_equal)
                    step(nc.vector.tensor_tensor(col[:, 2], top[:, :, 0], second, ALU.add))
                    step(nc.vector.reduce_sum(col[:, 0], gt[:], AX_X))
                    for j in range(TJ):
                        nc.vector.tensor_tensor_scan(rank[:, j], eq[:, j], eq[:, j], 0.0, ALU.add, ALU.max)
                    nc.vector.tensor_scalar(col[:, 2], col[:, 2], 1e-6, None, ALU.add)
                    step(nc.vector.tensor_scalar(col[:, 0], col[:, 0], -1.0, 2.0, ALU.mult, ALU.add))
                    nc.vector.reciprocal(col[:, 3], col[:, 2])
                    step(nc.vector.tensor_tensor(rank[:], rank[:], wide(col[:, 0]), ALU.is_le))
                    step(nc.vector.tensor_tensor(rank[:], rank[:], eq[:], ALU.mult))
                    step(nc.vector.tensor_tensor(gt[:], gt[:], rank[:], ALU.add))
                    step(nc.vector.tensor_tensor(gt[:], gt[:], prob[:], ALU.mult))
                    step(nc.vector.tensor_tensor(comb[:, s], gt[:], wide(col[:, 3]), ALU.mult))
                    assert done[0] == FRONT

                def h(ch, e, p):
                    dve.wait_ge(silu_done, ch * ITEMS + e + 1)
                    dve.wait_ge(yd_ready, ch * ITEMS + e - 1 + 2)
                    nc.vector.tensor_tensor(hh[:, e % 2], sg[:, e % 2], gu[:, p % 2, 1], ALU.mult).then_inc(h_ready, 1)

                def add_y(ch, e, s):
                    dve.wait_ge(yd_ready, ch * ITEMS + e + 1 + 2)
                    for j in range(TJ):
                        if e < EXPERTS:
                            last = nc.vector.scalar_tensor_tensor(ysum[:, j], yd[:, e % 2, j], comb[:, s, j, e:e + 1], ysum[:, j], ALU.mult, ALU.add)
                        else:
                            last = nc.vector.tensor_tensor(ysum[:, j], yd[:, e % 2, j], ysum[:, j], ALU.add)
                    last.then_inc(yd_free, 1)
                    dve.wait_ge(yd_free, ch * ITEMS + e + 1 + 2)

                def chunk(ch, b, cc, s, nxt):
                    base = ch * PER + FRONT
                    for e in range(ITEMS):
                        p = place(e) if nxt else e
                        h(ch, e, p)
                        if e == 0:
                            dve.wait_ge(x1_ready, ch + 1)
                            for j in range(TJ):
                                last = nc.vector.scalar_tensor_tensor(ysum[:, j], x1[:, s, j], comb[:, s, j, EXPERTS:EXPERTS + 1], x1[:, s, j],
                                                                      ALU.mult, ALU.add)
                            last.then_inc(seq, 1)
                            dve.wait_ge(seq, base + 1)
                        else:
                            add_y(ch, e - 1, s)
                        if nxt:
                            nb, ncc = (b, cc + 1) if cc < CPB - 1 else (b + 1, 0)
                            if e == 3:
                                front_a(ch + 1, nb, ncc, 1 - s, base + 1)
                            if e == 5:
                                front_b(ch + 1, 1 - s, base + 1)
                            if e == ROUTE_AFTER:
                                front_c(ch + 1, 1 - s, base + 1, FIRST + ch * RING + ROUTE, ROUTE % 2)
                            if e == 12:
                                front_d(ch + 1, 1 - s, base + 1)
                    add_y(ch, ITEMS - 1, s)
                    after = base + 1 + (FRONT if nxt else 0)
                    variance(ysum[:], 1, after + 1).then_inc(var2, 1)
                    dve.wait_ge(std2, ch + 1)
                    dve.wait_ge(y_out[s], (b * 2 + cc // 2 + 1) * 16)
                    normalise(y[:, s], ysum[:], 1, after + 2).then_inc(y_ready, 1)
                    dve.wait_ge(y_ready, ch + 1)

                front_a(0, 0, 0, 0, 0)
                front_b(0, 0, 0)
                front_c(0, 0, 0, 1, 1)
                front_d(0, 0, 0)
                with dve.Fori(0, BATCH - 1) as b:
                    for cc in range(CPB):
                        chunk(b * CPB + cc, b, cc, cc % 2, True)
                for cc in range(CPB):
                    chunk(NCHUNK - CPB + cc, BATCH - 1, cc, cc % 2, cc < CPB - 1)

            @block.tensor
            def _(pe):
                pe.sem_inc(yd_ready, 2)
                pe.wait_ge(consts, 5)

                def front_turn(ch, s, slot):
                    pe.wait_ge(x1_ready, ch + 1)
                    for a in range(HALVES):
                        for j in range(TJ):
                            last = nc.tensor.transpose(gu[:, slot, a, j * P:(j + 1) * P], x1[:, s, j, a * P:(a + 1) * P], identity[:])
                    last.then_inc(gu_ready, 1)

                def front_route(ch, s, slot):
                    pe.wait_ge(xt_ready, ch + 1)
                    for j in range(TJ):
                        o = gu[:, slot, 0, j * HEADS:(j + 1) * HEADS]
                        for a in range(HALVES):
                            c0 = TAPS - 1 + j * P
                            nc.tensor.matmul(o, xT[:, s, a, c0:c0 + P], router_w[:, a], start=(a == 0), stop=False)
                        last = nc.tensor.matmul(o, ones[:], router_b[:], start=False, stop=True)
                    last.then_inc(gu_ready, 1)

                def item_read(ch, e):
                    pe.wait_ge(h_ready, ch * ITEMS + e + 1 + 2)

                def up(ch, s, e, p, nxt):
                    if nxt and p - 2 == TURN:
                        pe.wait_ge(xt_ready, ch + 2)
                    elif nxt and p - 2 == ROUTE:
                        pe.wait_ge(logit_ready, ch + 2)
                    else:
                        item_read(ch, e - 1 if nxt and p - 1 in (TURN, ROUTE) else e - 2)
                    if e == 0:
                        pe.wait_ge(logit_ready, ch + 1)
                    g, u = gu[:, p % 2, 0], gu[:, p % 2, 1]
                    now = slice(TAPS - 1, TAPS - 1 + CHUNK)
                    if e < EXPERTS:
                        for a in range(HALVES):
                            nc.tensor.matmul(g, gate_w[:, e, a], xT[:, s, a, now], start=(a == 0), stop=(a == 1))
                        for a in range(HALVES):
                            last = nc.tensor.matmul(u, up_w[:, e, a], xT[:, s, a, now], start=(a == 0), stop=(a == 1))
                    else:
                        for k in range(TAPS):
                            for a in range(HALVES):
                                nc.tensor.matmul(g, conv_w[:, k, a], xT[:, s, a, k:k + CHUNK], start=(k + a == 0),
                                                 stop=(k == TAPS - 1 and a == 1))
                        for a in range(HALVES):
                            last = nc.tensor.matmul(u, sup_w[:, a], xT[:, s, a, now], start=(a == 0), stop=(a == 1))
                    last.then_inc(gu_ready, 1)

                def down(ch, e):
                    pe.wait_ge(h_ready, ch * ITEMS + e + 1 + 2)
                    pe.wait_ge(yd_free, ch * ITEMS + e + 1)
                    w = down_w[:, e] if e < EXPERTS else sdown_w[:]
                    for j in range(TJ):
                        last = nc.tensor.matmul(yd[:, e % 2, j], hh[:, e % 2, j * P:(j + 1) * P], w, start=True, stop=True)
                    last.then_inc(yd_ready, 1)

                def chunk(ch, s, nxt):
                    for e in range(ITEMS):
                        p = place(e) if nxt else e
                        up(ch, s, e, p, nxt)
                        if e:
                            down(ch, e - 1)
                        if nxt and e == TURN_AFTER:
                            item_read(ch, TURN_AFTER - 1)
                            front_turn(ch + 1, 1 - s, TURN % 2)
                        if nxt and e == ROUTE_AFTER:
                            item_read(ch, ROUTE_AFTER - 1)
                            front_route(ch + 1, 1 - s, ROUTE % 2)
                    down(ch, ITEMS - 1)

                front_turn(0, 0, 0)
                pe.wait_ge(w_in, 16 * 8)
                front_route(0, 0, 1)
                with pe.Fori(0, BATCH - 1) as b:
                    for cc in range(CPB):
                        chunk(b * CPB + cc, cc % 2, True)
                for cc in range(CPB):
                    chunk(NCHUNK - CPB + cc, cc % 2, cc < CPB - 1)


def scratch(nc):
    def dram(name, shape, dt=F32):
        return nc.dram_tensor(name, shape, dt).ap()

    return {
        "q": dram("s_q", [3, NH * HD, SEQ], BF16),
        "k": dram("s_k", [3, NH * HD, SEQ], BF16),
        "v": dram("s_v", [NH, P, KT, VW]),
        "vlow": dram("s_vlow", [NH, NBLK, VW]),
        "low": dram("s_low", [NH, NBLK, NBLK]),
        "lowm": dram("s_lowm", [NH, NBLK, NBLK]),
        "mask": dram("s_mask", [NH, NBLK, NBLK], BF16),
        "rm": dram("s_rm", [4, NH, KT]),
    }


_IN = {
    "xt": [NCHUNK, P, HALVES, CHUNK], "x": [BATCH * SEQ, D],
    "wq": [P, HALVES, D], "wk": [P, HALVES, D], "wv": [P, HALVES, D],
    "bias_qk": [P, 2, HALVES], "bias_head": [HD, 2, HEADS], "bv": [1, D],
    "router": [P, HALVES, HEADS], "router_bias": [1, HEADS],
    "gate": [P, EXPERTS, HALVES, INNER], "up": [P, EXPERTS, HALVES, INNER], "down": [INNER, EXPERTS, D],
    "conv": [P, TAPS, HALVES, INNER], "shared_up": [P, HALVES, INNER], "shared_down": [INNER, D],
}


def build(nc, t, out):
    scr = scratch(nc)
    prepare(nc, t, scr)
    with ExitStack() as ctx:
        att = ctx.enter_context(nc.sbuf_tensor("att", [P, NH, KT, HD], F32))
        gate_w, up_w = (ctx.enter_context(nc.sbuf_tensor(n, [P, EXPERTS, HALVES, INNER], F32)) for n in ("gate_w", "up_w"))
        w_in = ctx.enter_context(nc.semaphore("ffn_w_in"))
        attend(nc, t, scr, att, ((gate_w, "gate", w_in), (up_w, "up", w_in)))
        ffn(nc, t, att, out, gate_w, up_w, w_in)


def kernel(L0_attn_X, L0_attn_Wq, L0_attn_bq, L0_attn_Wk, L0_attn_bk, L0_attn_Wv, L0_attn_bv, L0_ffn_router_w,
           L0_ffn_router_bias, L0_ffn_expert_gate_w, L0_ffn_expert_up_w, L0_ffn_expert_down_w, L0_ffn_conv_w,
           L0_ffn_shared_up_w, L0_ffn_shared_down_w):
    import numpy as np
    import concourse.bacc as bacc
    from concourse.bass_utils import run_bass_kernel_spmd

    def rows(w):
        return np.asarray(w).reshape(HALVES, P, -1).transpose(1, 0, 2)

    def experts(w):
        return np.asarray(w).reshape(EXPERTS, HALVES, P, INNER).transpose(2, 0, 1, 3)

    x, bq, bk = (np.asarray(a) for a in (L0_attn_X, L0_attn_bq, L0_attn_bk))
    arrays = {
        "xt": x.reshape(NCHUNK, CHUNK, HALVES, P).transpose(0, 3, 2, 1),
        "x": x.reshape(BATCH * SEQ, D),
        "wq": rows(np.asarray(L0_attn_Wq).T), "wk": rows(np.asarray(L0_attn_Wk).T), "wv": rows(np.asarray(L0_attn_Wv).T),
        "bias_qk": np.stack([bq.reshape(HALVES, P).T, bk.reshape(HALVES, P).T], axis=1),
        "bias_head": np.stack([bq.reshape(HEADS, HD).T, bk.reshape(HEADS, HD).T], axis=1),
        "bv": np.asarray(L0_attn_bv).reshape(1, D),
        "router": rows(L0_ffn_router_w), "router_bias": np.asarray(L0_ffn_router_bias).reshape(1, HEADS),
        "gate": experts(L0_ffn_expert_gate_w), "up": experts(L0_ffn_expert_up_w),
        "down": np.asarray(L0_ffn_expert_down_w).transpose(1, 0, 2),
        "conv": np.asarray(L0_ffn_conv_w).transpose(2, 1, 0).reshape(TAPS, HALVES, P, INNER).transpose(2, 0, 1, 3),
        "shared_up": rows(L0_ffn_shared_up_w), "shared_down": np.asarray(L0_ffn_shared_down_w),
    }
    arrays = {"in_" + n: np.ascontiguousarray(a) for n, a in arrays.items()}
    nc = bacc.Bacc("TRN2", target_bir_lowering=False, num_devices=1)
    t = {n: nc.dram_tensor("in_" + n, shape, F32, kind="ExternalInput").ap() for n, shape in _IN.items()}
    out = nc.dram_tensor("out", [BATCH * SEQ, D], F32, kind="ExternalOutput").ap()
    build(nc, t, out)
    r = run_bass_kernel_spmd(nc, [arrays], core_ids=[0])
    return r.results[0]["out"].reshape(BATCH, SEQ, D)
```
